# Optimizing a Trainium2 kernel written in Bass

```python
import numpy as np
import jax
import jax.numpy as jnp

def _softmax(x, axis=-1):
    return jax.nn.softmax(x, axis=axis)

def _gelu(x):
    return jax.nn.gelu(x, approximate=True)

def _silu(x):
    return jax.nn.silu(x)

def _sigmoid(x):
    return jax.nn.sigmoid(x)

def _layernorm(x, axis=-1, eps=1e-05):
    m = jnp.mean(x, axis=axis, keepdims=True)
    v = jnp.var(x, axis=axis, keepdims=True)
    return (x - m) / jnp.sqrt(v + eps)

def _scatter_add(tgt, idx, src, axis=0):
    return tgt.at[idx].add(src)

def _segment_sum(src, seg, n):
    return jax.ops.segment_sum(src, seg, n)
kernel_name = 'mk_cond_seq_d4_seqx_r8_014b35'

def setup_inputs(seed: int=0):
    np.random.seed(seed)
    _w = jnp.asarray

    def _rec_inputs():
        import jax
        import jax.numpy as jnp
        _rk = jax.random.key(seed)
        x = -1.528e-05 + 0.9999 * jax.random.normal(jax.random.fold_in(_rk, 1), (128, 32, 256), jnp.float32)
        _lenS = 32 - jax.random.randint(jax.random.fold_in(_rk, 7), (128,), 0, max(1, 32 // 4) + 1, jnp.int32)
        _lenS2 = 32 - jax.random.randint(jax.random.fold_in(_rk, 8), (128,), 0, max(1, 32 // 4) + 1, jnp.int32)
        itok_B_1_2 = jax.random.randint(jax.random.fold_in(_rk, 11), (128,), 1, 3, jnp.int32)
        itok_B_17_1546 = jax.random.randint(jax.random.fold_in(_rk, 13), (128,), 17, 1547, jnp.int32)
        return (x, itok_B_1_2, itok_B_17_1546, _lenS)
    x, itok_B_1_2, itok_B_17_1546, _lenS = _rec_inputs()

    def _L0_cond_setup():
        import jax, jax.numpy as jnp
        import numpy as np
        H = 256
        K = 128
        R = 3
        B = 8
        S = 256
        LN_EPS = 1e-05
        key = jax.random.key(seed)
        ks = jax.random.split(key, 8)
        sd_d = 1.0 / np.sqrt(H)
        sd_u = 1.0 / np.sqrt(K)
        return {'role': jax.random.randint(ks[0], (B,), 0, R), 'hidden_states': jax.random.normal(ks[1], (B, S, H), dtype=jnp.float32), 'W_down': jax.random.uniform(ks[2], (R, H, K), jnp.float32, -sd_d, sd_d), 'b_down': jax.random.uniform(ks[3], (R, K), jnp.float32, -sd_d, sd_d), 'W_up': jax.random.uniform(ks[4], (R, K, H), jnp.float32, -sd_u, sd_u), 'b_up': jax.random.uniform(ks[5], (R, H), jnp.float32, -sd_u, sd_u), 'gamma': jnp.ones((R, H), jnp.float32), 'beta': jnp.zeros((R, H), jnp.float32)}
    _L0_cond_all = _L0_cond_setup()
    _L0_cond_in = {k: v for k, v in _L0_cond_all.items() if k in ('W_down', 'b_down', 'W_up', 'b_up', 'gamma', 'beta')}
    del _L0_cond_all

    def _L1_cond_setup():
        import jax, jax.numpy as jnp
        import numpy as np
        B, T, V = (8, 64, 256)
        H = 4 * V
        key = jax.random.key(seed)
        ks = jax.random.split(key, 16)
        s = lambda n: 1.0 / np.sqrt(n)
        inp = {'x': jax.random.uniform(ks[0], (B, T, V), dtype=jnp.float32), 'lens': jax.random.randint(ks[1], (B,), 1, T, dtype=jnp.int64), 'target_codes': jax.random.randint(ks[2], (B,), 0, V, dtype=jnp.int64), 'Wq': jax.random.normal(ks[3], (V, V), jnp.float32) * s(V), 'Wk': jax.random.normal(ks[4], (V, V), jnp.float32) * s(V), 'Wv': jax.random.normal(ks[5], (V, V), jnp.float32) * s(V), 'Wp': jax.random.normal(ks[6], (V, V), jnp.float32) * s(V), 'bp': jnp.zeros((V,), jnp.float32), 'cW1': jax.random.normal(ks[7], (V, H), jnp.float32) * s(V), 'cb1': jnp.zeros((H,), jnp.float32), 'cW2': jax.random.normal(ks[8], (H, V), jnp.float32) * s(H), 'cb2': jnp.zeros((V,), jnp.float32), 'mW1': jax.random.normal(ks[9], (2 * V, H), jnp.float32) * s(2 * V), 'mb1': jnp.zeros((H,), jnp.float32), 'mW2': jax.random.normal(ks[10], (H, V), jnp.float32) * s(H), 'mb2': jnp.zeros((V,), jnp.float32)}
        return inp
    _L1_cond_all = _L1_cond_setup()
    _L1_cond_in = {k: v for k, v in _L1_cond_all.items() if k in ('Wq', 'Wk', 'Wv', 'Wp', 'bp', 'cW1', 'cb1', 'cW2', 'cb2', 'mW1', 'mb1', 'mW2', 'mb2')}
    del _L1_cond_all

    def _L2_cond_setup():
        import jax, jax.numpy as jnp
        import numpy as np
        B, T, V = (8, 64, 256)
        H = 4 * V
        key = jax.random.key(seed)
        ks = jax.random.split(key, 16)
        s = lambda n: 1.0 / np.sqrt(n)
        inp = {'x': jax.random.uniform(ks[0], (B, T, V), dtype=jnp.float32), 'lens': jax.random.randint(ks[1], (B,), 1, T, dtype=jnp.int64), 'target_codes': jax.random.randint(ks[2], (B,), 0, V, dtype=jnp.int64), 'Wq': jax.random.normal(ks[3], (V, V), jnp.float32) * s(V), 'Wk': jax.random.normal(ks[4], (V, V), jnp.float32) * s(V), 'Wv': jax.random.normal(ks[5], (V, V), jnp.float32) * s(V), 'Wp': jax.random.normal(ks[6], (V, V), jnp.float32) * s(V), 'bp': jnp.zeros((V,), jnp.float32), 'cW1': jax.random.normal(ks[7], (V, H), jnp.float32) * s(V), 'cb1': jnp.zeros((H,), jnp.float32), 'cW2': jax.random.normal(ks[8], (H, V), jnp.float32) * s(H), 'cb2': jnp.zeros((V,), jnp.float32), 'mW1': jax.random.normal(ks[9], (2 * V, H), jnp.float32) * s(2 * V), 'mb1': jnp.zeros((H,), jnp.float32), 'mW2': jax.random.normal(ks[10], (H, V), jnp.float32) * s(H), 'mb2': jnp.zeros((V,), jnp.float32)}
        return inp
    _L2_cond_all = _L2_cond_setup()
    _L2_cond_in = {k: v for k, v in _L2_cond_all.items() if k in ('Wq', 'Wk', 'Wv', 'Wp', 'bp', 'cW1', 'cb1', 'cW2', 'cb2', 'mW1', 'mb1', 'mW2', 'mb2')}
    del _L2_cond_all

    def _L3_cond_setup():
        import jax, jax.numpy as jnp
        import numpy as np
        B, S, H = (8, 256, 256)
        BN = 128
        E = 3
        LN_EPS = 1e-05
        key = jax.random.key(seed)
        ks = jax.random.split(key, 8)
        stream = jax.random.randint(ks[0], (B,), 0, E, dtype=jnp.int32)
        hidden_states = jax.random.normal(ks[1], (B, S, H), dtype=jnp.float32)
        W_down = jax.random.normal(ks[2], (E, H, BN), dtype=jnp.float32) * 0.02
        b_down = jnp.zeros((E, BN), dtype=jnp.float32)
        W_up = jax.random.normal(ks[3], (E, BN, H), dtype=jnp.float32) * 0.02
        b_up = jnp.zeros((E, H), dtype=jnp.float32)
        ln_w = jnp.ones((E, H), dtype=jnp.float32)
        ln_b = jnp.zeros((E, H), dtype=jnp.float32)
        return {'stream': stream, 'hidden_states': hidden_states, 'W_down': W_down, 'b_down': b_down, 'W_up': W_up, 'b_up': b_up, 'ln_w': ln_w, 'ln_b': ln_b}
    _L3_cond_all = _L3_cond_setup()
    _L3_cond_in = {k: v for k, v in _L3_cond_all.items() if k in ('W_down', 'b_down', 'W_up', 'b_up', 'ln_w', 'ln_b')}
    del _L3_cond_all
    return {'x': x, 'itok_B_1_2': itok_B_1_2, 'itok_B_17_1546': itok_B_17_1546, '_lenS': _lenS, 'L0_cond_W_down': _L0_cond_in['W_down'], 'L0_cond_b_down': _L0_cond_in['b_down'], 'L0_cond_W_up': _L0_cond_in['W_up'], 'L0_cond_b_up': _L0_cond_in['b_up'], 'L0_cond_gamma': _L0_cond_in['gamma'], 'L0_cond_beta': _L0_cond_in['beta'], 'L1_cond_Wq': _L1_cond_in['Wq'], 'L1_cond_Wk': _L1_cond_in['Wk'], 'L1_cond_Wv': _L1_cond_in['Wv'], 'L1_cond_Wp': _L1_cond_in['Wp'], 'L1_cond_bp': _L1_cond_in['bp'], 'L1_cond_cW1': _L1_cond_in['cW1'], 'L1_cond_cb1': _L1_cond_in['cb1'], 'L1_cond_cW2': _L1_cond_in['cW2'], 'L1_cond_cb2': _L1_cond_in['cb2'], 'L1_cond_mW1': _L1_cond_in['mW1'], 'L1_cond_mb1': _L1_cond_in['mb1'], 'L1_cond_mW2': _L1_cond_in['mW2'], 'L1_cond_mb2': _L1_cond_in['mb2'], 'L2_cond_Wq': _L2_cond_in['Wq'], 'L2_cond_Wk': _L2_cond_in['Wk'], 'L2_cond_Wv': _L2_cond_in['Wv'], 'L2_cond_Wp': _L2_cond_in['Wp'], 'L2_cond_bp': _L2_cond_in['bp'], 'L2_cond_cW1': _L2_cond_in['cW1'], 'L2_cond_cb1': _L2_cond_in['cb1'], 'L2_cond_cW2': _L2_cond_in['cW2'], 'L2_cond_cb2': _L2_cond_in['cb2'], 'L2_cond_mW1': _L2_cond_in['mW1'], 'L2_cond_mb1': _L2_cond_in['mb1'], 'L2_cond_mW2': _L2_cond_in['mW2'], 'L2_cond_mb2': _L2_cond_in['mb2'], 'L3_cond_W_down': _L3_cond_in['W_down'], 'L3_cond_b_down': _L3_cond_in['b_down'], 'L3_cond_W_up': _L3_cond_in['W_up'], 'L3_cond_b_up': _L3_cond_in['b_up'], 'L3_cond_ln_w': _L3_cond_in['ln_w'], 'L3_cond_ln_b': _L3_cond_in['ln_b']}

def reference(x, itok_B_1_2, itok_B_17_1546, _lenS, L0_cond_W_down, L0_cond_b_down, L0_cond_W_up, L0_cond_b_up, L0_cond_gamma, L0_cond_beta, L1_cond_Wq, L1_cond_Wk, L1_cond_Wv, L1_cond_Wp, L1_cond_bp, L1_cond_cW1, L1_cond_cb1, L1_cond_cW2, L1_cond_cb2, L1_cond_mW1, L1_cond_mb1, L1_cond_mW2, L1_cond_mb2, L2_cond_Wq, L2_cond_Wk, L2_cond_Wv, L2_cond_Wp, L2_cond_bp, L2_cond_cW1, L2_cond_cb1, L2_cond_cW2, L2_cond_cb2, L2_cond_mW1, L2_cond_mb1, L2_cond_mW2, L2_cond_mb2, L3_cond_W_down, L3_cond_b_down, L3_cond_W_up, L3_cond_b_up, L3_cond_ln_w, L3_cond_ln_b):
    import jax
    import jax.numpy as jnp

    def _L0_cond_ref(role, hidden_states, W_down, b_down, W_up, b_up, gamma, beta):
        import jax, jax.numpy as jnp
        import numpy as np
        H = 256
        K = 128
        R = 3
        B = 8
        S = 256
        LN_EPS = 1e-05
        h = jnp.einsum('bsh,bhk->bsk', hidden_states, W_down[role]) + b_down[role][:, None, :]
        h = jax.nn.gelu(h, approximate=False)
        u = jnp.einsum('bsk,bkh->bsh', h, W_up[role]) + b_up[role][:, None, :]
        y = hidden_states + u
        mean = jnp.mean(y, axis=-1, keepdims=True)
        var = jnp.mean(jnp.square(y - mean), axis=-1, keepdims=True)
        yn = (y - mean) * jax.lax.rsqrt(var + LN_EPS)
        return yn * gamma[role][:, None, :] + beta[role][:, None, :]

    def _L1_cond_ref(x, lens, target_codes, Wq, Wk, Wv, Wp, bp, cW1, cb1, cW2, cb2, mW1, mb1, mW2, mb2):
        import jax, jax.numpy as jnp
        import numpy as np
        B, T, V = (8, 64, 256)
        H = 4 * V
        scale = V ** (-0.5)
        q = x @ Wq
        k = x @ Wk
        v = x @ Wv
        attn = jnp.einsum('btd,bTd->btT', q, k) * scale
        attn = jax.nn.softmax(attn, axis=-1)
        attn_out = jnp.einsum('btT,bTd->btd', attn, v) @ Wp + bp
        target_embed = jax.nn.one_hot(target_codes, V, dtype=x.dtype)[:, None, :]
        cms_out = jax.nn.gelu(attn_out @ cW1 + cb1, approximate=False) @ cW2 + cb2
        cms_out = cms_out + target_embed
        concat = jnp.concatenate([attn_out, cms_out], axis=-1)
        modifier = jax.nn.gelu(concat @ mW1 + mb1, approximate=False) @ mW2 + mb2
        out = jnp.clip(x + cms_out + modifier, 0.0, 1.0)
        return out

    def _L2_cond_ref(x, lens, target_codes, Wq, Wk, Wv, Wp, bp, cW1, cb1, cW2, cb2, mW1, mb1, mW2, mb2):
        import jax, jax.numpy as jnp
        import numpy as np
        B, T, V = (8, 64, 256)
        H = 4 * V
        scale = V ** (-0.5)
        q = x @ Wq
        k = x @ Wk
        v = x @ Wv
        attn = jnp.einsum('btd,bTd->btT', q, k) * scale
        attn = jax.nn.softmax(attn, axis=-1)
        attn_out = jnp.einsum('btT,bTd->btd', attn, v) @ Wp + bp
        target_embed = jax.nn.one_hot(target_codes, V, dtype=x.dtype)[:, None, :]
        cms_out = jax.nn.gelu(attn_out @ cW1 + cb1, approximate=False) @ cW2 + cb2
        cms_out = cms_out + target_embed
        concat = jnp.concatenate([attn_out, cms_out], axis=-1)
        modifier = jax.nn.gelu(concat @ mW1 + mb1, approximate=False) @ mW2 + mb2
        out = jnp.clip(x + cms_out + modifier, 0.0, 1.0)
        return out

    def _L3_cond_ref(stream, hidden_states, W_down, b_down, W_up, b_up, ln_w, ln_b):
        import jax, jax.numpy as jnp
        import numpy as np
        B, S, H = (8, 256, 256)
        BN = 128
        E = 3
        LN_EPS = 1e-05
        Wd = W_down[stream]
        bd = b_down[stream]
        Wu = W_up[stream]
        bu = b_up[stream]
        g = ln_w[stream]
        b = ln_b[stream]
        residual = hidden_states
        h = jnp.einsum('bsh,bhk->bsk', hidden_states, Wd) + bd[:, None, :]
        h = jax.nn.gelu(h, approximate=False)
        h = jnp.einsum('bsk,bkh->bsh', h, Wu) + bu[:, None, :]
        h = residual + h
        mean = jnp.mean(h, axis=-1, keepdims=True)
        var = jnp.mean(jnp.square(h - mean), axis=-1, keepdims=True)
        h = (h - mean) * jax.lax.rsqrt(var + LN_EPS)
        return h * g[:, None, :] + b[:, None, :]
    x = _L0_cond_ref(itok_B_1_2, x, L0_cond_W_down, L0_cond_b_down, L0_cond_W_up, L0_cond_b_up, L0_cond_gamma, L0_cond_beta)
    x = _L1_cond_ref(x, _lenS, itok_B_17_1546, L1_cond_Wq, L1_cond_Wk, L1_cond_Wv, L1_cond_Wp, L1_cond_bp, L1_cond_cW1, L1_cond_cb1, L1_cond_cW2, L1_cond_cb2, L1_cond_mW1, L1_cond_mb1, L1_cond_mW2, L1_cond_mb2)
    x = _L2_cond_ref(x, _lenS, itok_B_17_1546, L2_cond_Wq, L2_cond_Wk, L2_cond_Wv, L2_cond_Wp, L2_cond_bp, L2_cond_cW1, L2_cond_cb1, L2_cond_cW2, L2_cond_cb2, L2_cond_mW1, L2_cond_mb1, L2_cond_mW2, L2_cond_mb2)
    x = _L3_cond_ref(itok_B_1_2, x, L3_cond_W_down, L3_cond_b_down, L3_cond_W_up, L3_cond_b_up, L3_cond_ln_w, L3_cond_ln_b)
    return x

_drawn_inputs = setup_inputs


def setup_inputs(seed=0):
    import zlib

    import numpy as np

    out = dict(_drawn_inputs(seed))
    spreads = {'L0_cond_gamma': (1.0, 0.2),
     'L0_cond_beta': (0.0, 0.1),
     'L1_cond_bp': (0.0, 0.1),
     'L1_cond_cb1': (0.0, 0.1),
     'L1_cond_cb2': (0.0, 0.1),
     'L1_cond_mb1': (0.0, 0.1),
     'L1_cond_mb2': (0.0, 0.1),
     'L2_cond_bp': (0.0, 0.1),
     'L2_cond_cb1': (0.0, 0.1),
     'L2_cond_cb2': (0.0, 0.1),
     'L2_cond_mb1': (0.0, 0.1),
     'L2_cond_mb2': (0.0, 0.1),
     'L3_cond_b_down': (0.0, 0.283),
     'L3_cond_b_up': (0.0, 0.1),
     'L3_cond_ln_w': (1.0, 0.2),
     'L3_cond_ln_b': (0.0, 0.1)}
    factors = {'L0_cond_b_down': 2.864}
    for name, (base, spread) in spreads.items():
        noise = np.random.default_rng([zlib.crc32(name.encode()), seed]).standard_normal(out[name].shape)
        drawn = base * np.exp(spread * noise) if base else spread * noise
        out[name] = jnp.asarray(drawn.astype(out[name].dtype))
    for name, factor in factors.items():
        out[name] = (out[name] * factor).astype(out[name].dtype)
    return out
```

```python
from contextlib import ExitStack

import concourse.bass as bass
from concourse import mybir

F32 = mybir.dt.float32
F32R = mybir.dt.float32r
I32 = mybir.dt.int32
ALU = mybir.AluOpType
ACT = mybir.ActivationFunctionType
AXX = mybir.AxisListType.X

P = 128
HI, LO = 0, 1
SIDE = (5, 6, 7)
NEG = -3.0e38
EPS = 1e-5


def build(nc, x, role_ids, codes, l0, l1, l2, l3, out):
    NB, S, H = x.shape
    R, _, K = l0["W_down"].shape
    HID = l1["cW1"].shape[1]
    KT = H // P
    MT = HID // P
    T = 512
    G = T // P
    CB = T // S
    NC = NB * S // T
    QB = P // S
    TILES = 2 * MT
    SCALE = float(H) ** -0.5
    assert (K, KT, G, MT, QB) == (P, 2, 4, 8, 4)


    scratch = nc.dram_tensor("x_mid_dram", [NC, P, KT * T], F32, kind="Internal").ap()
    x_rows = x.rearrange("b s h -> (b s) h").rearrange("(c g p) h -> p c g h", g=G, p=P)
    out_rows = out.rearrange("b s h -> (b s) h").rearrange("(c g p) h -> p c g h", g=G, p=P)

    ctx = ExitStack()
    with ctx:
        def sb(name, shape, dt=F32):
            return ctx.enter_context(nc.sbuf_tensor(name, shape, dt))

        def sem(name):
            return ctx.enter_context(nc.semaphore(name))

        w_m = sb("w_m", [P, 2, KT, H], F32R)
        w_vp = sb("w_vp", [P, 2, KT, H], F32R)
        w_c1 = sb("w_c1", [P, 2, KT, HID], F32R)
        w_c2 = sb("w_c2", [P, 2, MT, H], F32R)
        w_m1 = sb("w_m1", [P, 2, 2 * KT, HID], F32R)
        w_m2 = sb("w_m2", [P, 2, MT, H], F32R)
        e_down = sb("e_down", [P, 2, KT, R, K], F32R)
        e_up = sb("e_up", [P, 2, R, H], F32R)
        stage = sb("stage", [P, 4, 512])

        ident = sb("ident", [P, P])
        ident_r = sb("ident_r", [P, P], F32R)
        block_mask = sb("block_mask", [P, P])
        mask_f = sb("mask_f", [P, R, NB])
        mask_r = sb("mask_r", [64, NB])
        mask_t = sb("mask_t", [P, R, NB // QB])
        one_hot = sb("one_hot", [P, KT, NB])
        g0_sel = sb("g0_sel", [P, KT, NB])
        b0_sel = sb("b0_sel", [P, KT, NB])
        bias = sb("bias", [P, 64])
        up_bias = [sb(f"up_bias{i}", [64, H], F32R) for i in range(2)]
        gb3 = sb("gb3", [64, 2 * H], F32R)
        index = sb("index", [P, 4])
        neg_half = sb("neg_half", [P, G])

        y = sb("y", [P, G, H])
        x_new = sb("x_new", [P, KT, T])
        x_mlp = sb("x_mlp", [P, KT, T])
        x_out = sb("x_out", [P, KT, T])
        x_t = sb("x_t", [P, 2, KT, T], F32R)
        a_t = sb("a_t", [P, 2, KT, T], F32R)
        v_t = sb("v_t", [P, 2, G, H], F32R)
        att = sb("att", [P, 2, KT, T], F32R)
        cms = sb("cms", [P, 2, KT, T], F32R)
        res = sb("res", [P, KT, T])
        gel = sb("gel", [P, 2, T])
        hid = sb("hid", [P, 2, 3, T], F32R)
        soft = sb("soft", [P, T])
        sel = sb("sel", [P, T])
        h_t = sb("h_t", [P, 2, T], F32R)
        masks = sb("masks", [64, T], F32R)
        s_max = sb("s_max", [P, G])
        s_sum = sb("s_sum", [P, G])
        s_inv = sb("s_inv", [P, G])
        stats = sb("stats", [P, G, 6])
        mean_var = sb("mean_var", [P, G, 2])
        var_eps = sb("var_eps", [P, G])
        rstd = sb("rstd", [P, G])
        p_t = a_t[:, :, 0, :]
        sel2 = soft

        bank = [ctx.enter_context(nc.psum_tensor(f"bank{i}", [P, 512], F32)) for i in range(8)]
        hid_bank, y_bank = bank[0:3], bank[3:5]
        S0, S1, S2 = (bank[i] for i in SIDE)

        ids_in, rows_in, bias_in = sem("ids_in"), sem("rows_in"), sem("bias_in")
        stage_in = [sem(f"stage_in{i}") for i in range(4)]
        raw_in, x_in, mid_in = sem("raw_in"), sem("x_in"), sem("mid_in")
        mid_stored, out_stored = sem("mid_stored"), sem("out_stored")
        pool_const, dve_const, pe_const = sem("pool_const"), sem("dve_const"), sem("pe_const")
        w_hi, w_lo, table_step = sem("w_hi"), sem("w_lo"), sem("table_step")
        prep_pe, prep_act, prep_dve = sem("prep_pe"), sem("prep_act"), sem("prep_dve")
        hid_mm, gelu_done, hid_hi, hid_lo, hid_used = (sem(n) for n in (
            "hid_mm", "gelu_done", "hid_hi", "hid_lo", "hid_used"))
        cms_f, cms_hi, cms_lo, res_done = (sem(n) for n in ("cms_f", "cms_hi", "cms_lo", "res_done"))
        out_sum, out_clip, moved = sem("out_sum"), sem("out_clip"), sem("moved")
        xa_hi, xa_lo, a_mm, a_hi, a_lo = (sem(n) for n in ("xa_hi", "xa_lo", "a_mm", "a_hi", "a_lo"))
        v_mm, v_hi, v_lo, score_mm, soft_dve, exp_done = (sem(n) for n in (
            "v_mm", "v_hi", "v_lo", "score_mm", "soft_dve", "exp_done"))
        p_mm, p_hi, p_lo, att_mm, att_hi, att_lo = (sem(n) for n in (
            "p_mm", "p_hi", "p_lo", "att_mm", "att_hi", "att_lo"))
        xin_mm, xh_hi, xh_lo, down_mm, sel_dve, sel_gelu, h_hi, h_lo = (sem(n) for n in (
            "xin_mm", "xh_hi", "xh_lo", "down_mm", "sel_dve", "sel_gelu", "h_hi", "h_lo"))
        masks_done, up_mm, y_acc, ln_stats, ln_aggr, ln_var, ln_rstd, y_norm = (sem(n) for n in (
            "masks_done", "up_mm", "y_acc", "ln_stats", "ln_aggr", "ln_var", "ln_rstd", "y_norm"))
        xt_mm, x_gamma, x_beta, gb_mm, gb_mul, gb_add = (sem(n) for n in (
            "xt_mm", "x_gamma", "x_beta", "gb_mm", "gb_mul", "gb_add"))

        CB1, MB1, BP, CB2, MB2, BD = 0, MT, 2 * MT, 2 * MT + 2, 2 * MT + 4, 2 * MT + 6

        def bias_col(block, col):
            return bias[:, 32 * block + col:32 * block + col + 1]

        def pieces(expert, layer):
            down = expert["W_down"].rearrange("r (t p) k -> t p r k", p=P)
            up = expert["W_up"].rearrange("r k h -> k r h")
            found = [(down[t], lambda s, t=t: e_down[:, s, t]) for t in range(KT)]
            found += [(up[:, :, P * t:P * t + P], lambda s, t=t: e_up[:, s, :, P * t:P * t + P])
                      for t in range(KT)]

            def wide(w, target):
                rows = w.rearrange("(t p) n -> t p n", p=P)
                return [(rows[t][:, n:n + 512].unsqueeze(1), lambda s, t=t, n=n: target[:, s, t:t + 1, n:n + 512])
                        for t in range(rows.shape[0]) for n in range(0, HID, 512)]

            def narrow(w, target):
                rows = w.rearrange("(t p) n -> p t n", p=P)
                return [(rows[:, t:t + 2, :], lambda s, t=t: target[:, s, t:t + 2, :]) for t in range(0, MT, 2)]

            return (found + wide(layer["cW1"], w_c1) + narrow(layer["cW2"], w_c2)
                    + wide(layer["mW1"], w_m1) + narrow(layer["mW2"], w_m2))

        PIECES = pieces(l0, l1) + pieces(l3, l2)
        NP = len(PIECES) // 2
        P_EXP, P_C1, P_C2, P_M1, P_M2 = 4, 8, 12, 20, 24
        assert NP == P_M2

        TABLES = 5 + R + 1 + KT + QB * R

        def stage_view(i):
            src = PIECES[i][0]
            a, b = src.shape[1], src.shape[2]
            return stage[:, i % 4, 0:a * b].rearrange("p (a b) -> p a b", b=b)

        def chunk_bc(table, c):
            part = table[:, bass.ds(c * CB, CB)] if not isinstance(c, int) else table[:, c * CB:c * CB + CB]
            return part.unsqueeze(2).broadcast_to([table.shape[0], CB, S])

        def tok(ap):
            return ap.rearrange("p (b s) -> p b s", s=S)

        def f(ap):
            return ap.bitcast(F32)

        def side(j, first):
            if first:
                t = j + 1 if not isinstance(j, int) or j + 1 < NC else None
                h = j + 2 if not isinstance(j, int) or j + 2 < NC else None
                return j + 1, t, h
            a = j + 1 if not isinstance(j, int) or j + 1 < 2 * NC else None
            t = j - 2 if not isinstance(j, int) or j - 2 >= NC else None
            h = j - 1 if not isinstance(j, int) or NC <= j - 1 < 2 * NC else None
            return a, t, h

        def run_slots(eng, slot):
            slot(-1, True)
            slot(0, True)
            with eng.Fori(1, NC - 2) as j:
                slot(j, True)
            slot(NC - 2, True)
            slot(NC - 1, True)
            slot(NC, False)
            slot(NC + 1, False)
            with eng.Fori(NC + 2, 2 * NC - 1) as j:
                slot(j, False)
            for j in range(2 * NC - 1, 2 * NC + 2):
                slot(j, False)

        def has_mlp(j):
            return not isinstance(j, int) or 0 <= j < 2 * NC

        def not_first(j):
            return not isinstance(j, int) or j > 0

        block = ctx.enter_context(nc.Block())

        @block.sync
        def _(sp):
            def load_piece(i):
                if i >= 4:
                    sp.wait_ge(w_lo, i - 3)
                sp.dma_start(stage_view(i), PIECES[i][0]).then_inc(stage_in[i % 4], 16)

            def load_raw(n, w, k):
                if n >= 2:
                    sp.wait_ge(prep_pe, 4 * k + 1)
                sp.dma_start(x_out[:, n % 2, :].rearrange("p (t n) -> p t n", n=H),
                             w.rearrange("(t p) n -> p t n", p=P)).then_inc(raw_in, 16)

            def load_x(h):
                if not isinstance(h, int) or h > 0:
                    sp.wait_ge(xt_mm, KT * h)
                c = bass.ds(h, 1)
                sp.dma_start(y[:].unsqueeze(1), x_rows[:, c, :, :]).then_inc(x_in, 16)

            def load_mid(a):
                if isinstance(a, int):
                    sp.wait_ge(mid_stored, 16 * (NC if a > NC + 1 else NC - 1))
                sp.wait_ge(moved, a)
                sp.dma_start(x_new[:].unsqueeze(1), scratch.rearrange("c p (t n) -> p c t n", n=T)[:, bass.ds(a - NC, 1), :, :]
                             ).then_inc(mid_in, 16)

            def store_mid(j):
                sp.wait_ge(out_clip, KT * (j + 1))
                sp.dma_start(scratch.rearrange("c p (t n) -> p c t n", n=T)[:, bass.ds(j, 1), :, :],
                             x_out[:].unsqueeze(1)).then_inc(mid_stored, 16)

            def store_out(t):
                sp.wait_ge(gb_add, G * (t - NC + 1))
                sp.dma_start(out_rows[:, bass.ds(t - NC, 1), :, :], y[:].unsqueeze(1)).then_inc(out_stored, 16)

            ids = x_mlp[:, 1, :].bitcast(I32)
            sp.dma_start(ids[:, 0:NB], role_ids.partition_broadcast(P)).then_inc(ids_in, 16)
            sp.dma_start(ids[:, NB:2 * NB], codes.partition_broadcast(P)).then_inc(ids_in, 16)
            load_x(0)
            for i in range(4):
                load_piece(i)
            sp.wait_ge(dve_const, 2)
            for i, (l, e) in enumerate(((l1, l0), (l2, l3))):
                for col, name in ((CB1, "cb1"), (MB1, "mb1"), (BP, "bp"), (CB2, "cb2"), (MB2, "mb2")):
                    v = l[name].rearrange("(m p) -> m p", p=P)
                    sp.dma_start(gel[32 * i + col:32 * i + col + v.shape[0], 0, 0:P], v).then_inc(bias_in, 16)
                sp.dma_start(gel[32 * i + BD:32 * i + BD + R, 0, 0:P], e["b_down"]).then_inc(bias_in, 16)
            for n, name in enumerate(("Wq", "Wk")):
                load_raw(n, l1[name], 0)
            sp.dma_start(x_mlp[0:R, 0, 0:H], l0["gamma"]).then_inc(rows_in, 16)
            sp.dma_start(x_mlp[0:R, 0, H:2 * H], l0["beta"]).then_inc(rows_in, 16)
            for q in (0, 32):
                sp.dma_start(x_new[q:q + R, 0, 0:H], l3["gamma"]).then_inc(rows_in, 16)
                sp.dma_start(x_new[q:q + R, 0, H:2 * H], l3["beta"]).then_inc(rows_in, 16)
                sp.dma_start(x_new[q:q + R, 1, 0:H], l0["b_up"]).then_inc(rows_in, 16)
                sp.dma_start(x_new[q:q + R, 1, H:2 * H], l3["b_up"]).then_inc(rows_in, 16)
            for i in range(4, 8):
                load_piece(i)
            for n, name in ((2, "Wv"), (3, "Wp")):
                load_raw(n, l1[name], 0)
            for i in range(8, 16):
                load_piece(i)
            load_x(1)
            for i in range(16, NP):
                load_piece(i)

            def slot(j, first):
                a, t, h = side(j, first)
                if not first and t is not None:
                    store_out(t)
                if first and (not isinstance(j, int) or j + 2 < NC):
                    load_x(j + 2)
                if isinstance(j, int) and j == NC - 1:
                    for n, name in enumerate(("Wq", "Wk")):
                        if n == 0:
                            sp.wait_ge(mid_stored, 16 * (NC - 1))
                        load_raw(n, l2[name], 1)
                    for i in range(NP, NP + P_EXP):
                        load_piece(i)
                    for n, name in ((2, "Wv"), (3, "Wp")):
                        load_raw(n, l2[name], 1)
                    for i in range(NP + P_EXP, NP + P_C1):
                        load_piece(i)
                    load_mid(NC + 1)
                    for i in range(NP + P_C1, NP + P_M1):
                        load_piece(i)
                    store_mid(NC - 1)
                    for i in range(NP + P_M1, NP + P_M2):
                        load_piece(i)
                    return
                if first:
                    store_mid(j)
                if isinstance(j, int) and j == NC - 2:
                    load_mid(NC)
                if not first and (not isinstance(j, int) or j + 2 < 2 * NC):
                    load_mid(j + 2)

            slot(0, True)
            with sp.Fori(1, NC - 2) as j:
                slot(j, True)
            slot(NC - 2, True)
            slot(NC - 1, True)
            slot(NC, False)
            slot(NC + 1, False)
            with sp.Fori(NC + 2, 2 * NC - 2) as j:
                slot(j, False)
            for j in range(2 * NC - 2, 2 * NC + 2):
                slot(j, False)
            sp.wait_ge(mid_stored, 16 * NC)
            sp.wait_ge(out_stored, 16 * NC)

        @block.gpsimd
        def _(pool):
            chain = [0]

            def link(ins):
                chain[0] += 1
                ins.then_inc(pool_const, 1)
                pool.wait_ge(pool_const, chain[0])

            link(pool.memset(ident[:], 0.0))
            link(pool.affine_select(out=ident[:], in_=ident[:], compare_op=ALU.not_equal, fill=1.0, base=0,
                                    pattern=[[-1, P]], channel_multiplier=1))
            link(pool.memset(block_mask[:], NEG))
            for q in range(QB):
                link(pool.memset(block_mask[S * q:S * q + S, S * q:S * q + S], 0.0))
            link(pool.memset(neg_half[:], -0.5))
            for t in range(KT):
                link(pool.iota(index[:, t:t + 1], [[0, 1]], base=P * t, channel_multiplier=1,
                               allow_small_or_imprecise_dtypes=True))
            for q in (0, 32):
                link(pool.iota(index[q:q + 32, 2:3], [[0, 1]], base=0, channel_multiplier=1,
                               allow_small_or_imprecise_dtypes=True))
            pool.tensor_copy(ident_r[:], ident[:]).then_inc(pool_const, 1)

            def spread_masks(h, c, before):
                if not isinstance(h, int) or h > 0:
                    pool.wait_ge(up_mm, 8 * h)
                if before is not None:
                    pool.wait_ge(gb_mm, G * (before - NC + 1))
                part = chunk_bc(mask_r, c)
                pool.tensor_tensor(tok(masks[:]), part, part, ALU.mult).then_inc(masks_done, 1)

            def power(h):
                pool.wait_ge(ln_var, h + 1)
                pool.tensor_tensor(rstd[:], var_eps[:], neg_half[:], ALU.pow).then_inc(ln_rstd, 1)

            def add_beta(t):
                for m in range(KT):
                    pool.wait_ge(x_gamma, KT * t + m + 1)
                    pool.tensor_tensor(tok(x_new[:, m, :]), tok(x_new[:, m, :]), chunk_bc(b0_sel[:, m, :], t),
                                       ALU.add).then_inc(x_beta, 1)

            def residual(j):
                pool.wait_ge(moved, j + 1)
                pool.wait_ge(cms_hi, KT * (j + 1))
                for m in range(KT):
                    pool.wait_ge(cms_lo, KT * j + m + 1)
                    pool.tensor_tensor(res[:, m, :], res[:, m, :], x_mlp[:, m, :], ALU.add).then_inc(res_done, 1)

            def split_piece(i):
                src = stage_view(i)
                pool.wait_ge(stage_in[i % 4], 16 * (i // 4 + 1))
                pool.tensor_copy(PIECES[i][1](HI), src).then_inc(w_hi, 1)
                pool.wait_ge(w_hi, i + 1)
                pool.tensor_tensor(PIECES[i][1](LO), src, f(PIECES[i][1](HI)), ALU.subtract).then_inc(w_lo, 1)

            pool.wait_ge(table_step, TABLES)
            pool.wait_ge(pe_const, 2)
            spread_masks(0, 0, None)
            power(0)

            def slot(j, first):
                a, t, h = side(j, first)
                if first and t is not None:
                    add_beta(t)
                if isinstance(j, int) and j == NC - 1:
                    for i in range(NP, NP + P_EXP):
                        split_piece(i)
                if has_mlp(j):
                    residual(j)
                if h is not None:
                    c = h if first else h - NC
                    spread_masks(h, c, t if not first else None)
                    power(h)
                if isinstance(j, int) and j == NC - 1:
                    pool.wait_ge(hid_used, TILES * j + MT)
                    for i in range(NP + P_EXP, NP + P_C2):
                        split_piece(i)
                    pool.wait_ge(hid_mm, TILES * (j + 1))
                    for i in range(NP + P_C2, NP + P_M1):
                        split_piece(i)
                    pool.wait_ge(hid_used, TILES * (j + 1))
                    for i in range(NP + P_M1, NP + P_M2):
                        split_piece(i)

            run_slots(pool, slot)

        @block.scalar
        def _(act):
            def hi_piece(i):
                act.wait_ge(stage_in[i % 4], 16 * (i // 4 + 1))
                act.activation(PIECES[i][1](HI), stage_view(i), ACT.Identity).then_inc(w_hi, 1)

            def hi_prep(k, n, src):
                act.wait_ge(prep_pe, 4 * k + (2, 4)[n])
                act.activation((w_m, w_vp)[n][:, HI].rearrange("p t n -> p (t n)"), src[:],
                               ACT.Identity).then_inc(prep_act, 1)

            def hi_head_x(h, first, a):
                if first:
                    for m in range(KT):
                        act.wait_ge(xin_mm, KT * h + m + 1)
                        if a is not None:
                            act.wait_ge(v_mm, 2 * (a + 1))
                        act.activation(x_t[:, HI, m, :], (S1, S2)[m][:], ACT.Identity).then_inc(xh_hi, 1)
                    return
                act.wait_ge(out_clip, KT * (h + 1))
                act.wait_ge(v_mm, 2 * (a + 1) if a is not None else 4 * NC)
                act.wait_ge(up_mm, 8 * h)
                for m in range(KT):
                    act.activation(x_t[:, HI, m, :], x_out[:, m, :], ACT.Identity).then_inc(xh_hi, 1)

            def head_gelu(h):
                act.wait_ge(sel_dve, 5 * (h + 1))
                act.activation(sel[:], sel[:], ACT.Gelu).then_inc(sel_gelu, 1)
                act.wait_ge(sel_gelu, h + 1)
                if not isinstance(h, int) or h > 0:
                    act.wait_ge(up_mm, 8 * h)
                act.activation(h_t[:, HI, :], sel[:], ACT.Identity).then_inc(h_hi, 1)

            def hi_att_x(a, first, h_before):
                if first:
                    act.wait_ge(x_beta, KT * (a + 1))
                else:
                    act.wait_ge(mid_in, 16 * (a - NC + 1))
                if not isinstance(a, int) or a > 0:
                    act.wait_ge(v_mm, 2 * a)
                if h_before is not None:
                    act.wait_ge(up_mm, 8 * h_before + 2)
                for m in range(KT):
                    act.activation(x_t[:, HI, m, :], x_new[:, m, :], ACT.Identity).then_inc(xa_hi, 1)

            def hi_a(a):
                for m in range(KT):
                    act.wait_ge(a_mm, KT * a + m + 1)
                    act.activation(a_t[:, HI, m, :], (S2, S0)[m][:], ACT.Identity).then_inc(a_hi, 1)

            def exps(a):
                act.wait_ge(soft_dve, 6 * a + 3)
                act.activation(soft[:], soft[:], ACT.Exp).then_inc(exp_done, 1)

            def hi_v(a, n):
                act.wait_ge(v_mm, 2 * a + n + 1)
                act.activation(v_t[:, HI, 2 * n:2 * n + 2, :].rearrange("p g n -> p (g n)"), (S2, S0)[n][:],
                               ACT.Identity).then_inc(v_hi, 1)

            def hi_p(a):
                act.wait_ge(p_mm, a + 1)
                act.activation(p_t[:, HI, :], S0[:], ACT.Identity).then_inc(p_hi, 1)

            def hi_att(a, blk):
                for m in range(KT):
                    act.wait_ge(att_mm, KT * a + m + 1)
                    act.activation(att[:, HI, m, :], (S0, S1)[m][:], ACT.Identity,
                                   bias=bias_col(blk, BP + m)).then_inc(att_hi, 1)

            def gelu(j, n, blk):
                act.wait_ge(hid_mm, TILES * j + n + 1)
                if n >= 2 or not_first(j):
                    act.wait_ge(hid_lo, TILES * j + n - 1)
                col = CB1 + n if n < MT else MB1 + n - MT
                act.activation(gel[:, n % 2, :], hid_bank[n % 3][:], ACT.Gelu,
                               bias=bias_col(blk, col)).then_inc(gelu_done, 1)

            def hi_cms(j):
                for m in range(KT):
                    act.wait_ge(cms_f, KT * j + m + 1)
                    act.activation(cms[:, HI, m, :], res[:, m, :], ACT.Identity).then_inc(cms_hi, 1)

            def move(a):
                if not isinstance(a, int) or a > 0:
                    act.wait_ge(res_done, KT * a)
                act.wait_ge(xa_lo, KT * (a + 1))
                act.activation(x_mlp[:], x_new[:], ACT.Copy).then_inc(moved, 1)

            def slot(j, first):
                a, t, h = side(j, first)
                blk = 0 if first else 1
                ablk = 0 if first and not (isinstance(j, int) and j == NC - 1) else 1
                startup = isinstance(j, int) and j == -1
                turn = isinstance(j, int) and j == NC - 1
                mlp = has_mlp(j)
                h_before = j - 2 if not first and (not isinstance(j, int) or j >= NC + 2) else None
                for n in range(TILES):
                    if n == 2 and a is not None:
                        hi_att_x(a, not ablk, h_before)
                    if n == 12 and h is not None:
                        head_gelu(h)
                    if n == MT and a is not None:
                        exps(a)
                    if n == MT:
                        if a is not None:
                            hi_v(a, 0)
                        if mlp:
                            hi_cms(j)
                        if a is not None:
                            hi_v(a, 1)
                    if mlp:
                        gelu(j, n, blk)
                    if n == 1 and turn:
                        hi_prep(1, 0, S0)
                    if n == 3 and a is not None:
                        hi_a(a)
                    if n == 5 and turn:
                        hi_prep(1, 1, S2)
                    if n == 8 and h is not None:
                        hi_head_x(h, first, a)
                    if n == 9 and a is not None:
                        hi_p(a)
                        move(a)
                    if startup and n in (3, 5, 9, 12):
                        for i in {3: range(12, 14), 5: range(14, 16), 9: range(16, 20), 12: range(20, 24)}[n]:
                            hi_piece(i)
                if a is not None:
                    hi_att(a, ablk)

            hi_head_x(0, True, None)
            for i in range(8):
                hi_piece(i)
            hi_prep(0, 0, hid_bank[2])
            head_gelu(0)
            hi_prep(0, 1, hid_bank[1])
            for i in range(8, 12):
                hi_piece(i)
            run_slots(act, slot)

        @block.vector
        def _(dve):
            ids = x_mlp[:, 1, :].bitcast(I32)
            work = res
            dve.memset(gel[:, 0, 0:P], 0.0).then_inc(dve_const, 1)
            for r in (*up_bias, gb3):
                last = dve.memset(f(r[:]), 0.0)
            last.then_inc(dve_const, 1)
            chain = [0]

            def link(ins):
                chain[0] += 1
                ins.then_inc(table_step, 1)
                dve.wait_ge(table_step, chain[0])

            dve.wait_ge(ids_in, 32)
            dve.wait_ge(pool_const, 9 + QB)
            roles, code, tmp = work[:, 0, 0:NB], work[:, 0, NB:2 * NB], work[:, 0, 2 * NB:3 * NB]
            link(dve.tensor_copy(roles, ids[:, 0:NB]))
            link(dve.tensor_copy(code, ids[:, NB:2 * NB]))
            link(dve.tensor_scalar(tmp, roles, 0.0, float(R), ALU.is_lt, ALU.mult))
            link(dve.tensor_tensor(roles, roles, tmp, ALU.add))
            link(dve.tensor_scalar(roles, roles, 0.0, float(R - 1), ALU.max, ALU.min))
            for r in range(R):
                link(dve.tensor_scalar(mask_f[:, r, :], roles, float(r), None, ALU.is_equal))
            link(dve.tensor_scalar(mask_r[:], roles[0:64, :], index[0:64, 2:3], None, ALU.is_equal))
            for m in range(KT):
                link(dve.tensor_scalar(one_hot[:, m, :], code, index[:, m:m + 1], None, ALU.is_equal))
            for q in range(QB):
                for r in range(R):
                    link(dve.tensor_copy(mask_t[S * q:S * q + S, r, :],
                                         mask_f[S * q:S * q + S, r, :].rearrange("p (g q) -> p q g", q=QB)[:, q, :]))

            def lo_piece(i):
                dve.wait_ge(w_hi, i + 1)
                dve.tensor_tensor(PIECES[i][1](LO), stage_view(i), f(PIECES[i][1](HI)), ALU.subtract).then_inc(w_lo, 1)

            def prep_copy(k, n, src):
                dve.wait_ge(prep_pe, 4 * k + (1, 1, 3)[n])
                dve.tensor_copy(res[:, (0, 1, 0)[n], :], src[:]).then_inc(prep_dve, 1)

            def prep_lo(k, n, src):
                dve.wait_ge(prep_act, 2 * k + n + 1)
                w = (w_m, w_vp)[n]
                dve.tensor_tensor(w[:, LO].rearrange("p t n -> p (t n)"), src[:],
                                  f(w[:, HI].rearrange("p t n -> p (t n)")), ALU.subtract).then_inc(prep_dve, 1)

            def lo_head_x(h, first):
                for m in range(KT):
                    dve.wait_ge(xh_hi, KT * h + m + 1)
                    src = (S1, S2)[m][:] if first else x_out[:, m, :]
                    dve.tensor_tensor(x_t[:, LO, m, :], src, f(x_t[:, HI, m, :]), ALU.subtract).then_inc(xh_lo, 1)

            def select(h, first, a):
                c = h if first else h - NC
                blk = 0 if first else 1
                if a is not None:
                    dve.wait_ge(p_mm, a + 1)
                if not isinstance(h, int) or h > 0:
                    dve.wait_ge(h_lo, h)
                for r in range(R):
                    dve.wait_ge(down_mm, R * h + r + 1)
                    to = (sel, sel2, sel2)[r]
                    if r == 2:
                        dve.wait_ge(sel_dve, 5 * h + 3)
                    dve.scalar_tensor_tensor(out=tok(to[:]), in0=tok((S1, S2, S0)[r][:]), scalar=bias_col(blk, BD + r),
                                             in1=chunk_bc(mask_f[:, r, :], c), op0=ALU.add, op1=ALU.mult
                                             ).then_inc(sel_dve, 1)
                    if r:
                        dve.wait_ge(sel_dve, 5 * h + 2 * r)
                        dve.tensor_tensor(sel[:], sel[:], sel2[:], ALU.add).then_inc(sel_dve, 1)

            def lo_h(h):
                dve.wait_ge(h_hi, h + 1)
                dve.tensor_tensor(h_t[:, LO, :], sel[:], f(h_t[:, HI, :]), ALU.subtract).then_inc(h_lo, 1)

            UP_BANKS = (S1, S2, S0, S1, S2, S0, S1, S2)

            def accumulate(h, first, steps):
                for u in steps:
                    pair = u % 2
                    dve.wait_ge(up_mm, 8 * h + u + 1)
                    src = UP_BANKS[u]
                    yp = y[:, 2 * pair:2 * pair + 2, :].rearrange("p g n -> p (g n)")
                    if u < 2:
                        if first:
                            dve.wait_ge(x_in, 16 * (h + 1))
                            dve.tensor_tensor(yp, src[:], yp, ALU.add).then_inc(y_acc, 1)
                        else:
                            if not isinstance(h, int) or h > NC:
                                dve.wait_ge(out_stored, 16 * (h - NC))
                            dve.tensor_copy(yp, src[:]).then_inc(y_acc, 1)
                        continue
                    dve.wait_ge(y_acc, 8 * h + u - 1)
                    for i in range(2):
                        g = 2 * pair + i
                        c = (h if first else h - NC) * G + g
                        m = mask_t[:, u // 2 - 1, bass.ds(c, 1)]
                        last = dve.scalar_tensor_tensor(out=y[:, g, :], in0=src[:, i * H:(i + 1) * H], scalar=m,
                                                        in1=y[:, g, :], op0=ALU.mult, op1=ALU.add)
                    last.then_inc(y_acc, 1)

            def moments(h):
                for g in range(G):
                    dve.wait_ge(y_acc, 8 * h + 7 + g // 2)
                    dve.bn_stats(stats[:, g, :], y[:, g, :]).then_inc(ln_stats, 1)
                dve.wait_ge(ln_stats, G * (h + 1))
                dve.memset(var_eps[:], 0.0)
                for g in range(G):
                    dve.bn_aggr(mean_var[:, g, :], stats[:, g, :]).then_inc(ln_aggr, 1)
                dve.wait_ge(ln_aggr, G * (h + 1))
                dve.tensor_scalar(var_eps[:], mean_var[:, :, 1], EPS, None, ALU.add).then_inc(ln_var, 1)

            def normalize(h):
                dve.wait_ge(ln_rstd, h + 1)
                for g in range(G):
                    dve.tensor_scalar(y[:, g, :], y[:, g, :], mean_var[:, g, 0:1], rstd[:, g:g + 1],
                                      ALU.subtract, ALU.mult).then_inc(y_norm, 1)

            def tail_gamma(t):
                if not isinstance(t, int) or t > 0:
                    dve.wait_ge(moved, t)
                for m in range(KT):
                    dve.wait_ge(xt_mm, KT * t + m + 1)
                    dve.tensor_tensor(tok(x_new[:, m, :]), tok((S1, S2)[m][:]), chunk_bc(g0_sel[:, m, :], t),
                                      ALU.mult).then_inc(x_gamma, 1)

            def tail_out(t, gs):
                for g in gs:
                    dve.wait_ge(gb_mm, G * (t - NC) + g + 1)
                    src = (S1, S2, S0, S1)[g]
                    dve.tensor_tensor(y[:, g, :], y[:, g, :], src[:, 0:H], ALU.mult).then_inc(gb_mul, 1)
                    dve.wait_ge(gb_mul, G * (t - NC) + g + 1)
                    dve.tensor_tensor(y[:, g, :], y[:, g, :], src[:, H:2 * H], ALU.add).then_inc(gb_add, 1)

            def lo_att_x(a):
                for m in range(KT):
                    dve.wait_ge(xa_hi, KT * a + m + 1)
                    dve.tensor_tensor(x_t[:, LO, m, :], x_new[:, m, :], f(x_t[:, HI, m, :]), ALU.subtract
                                      ).then_inc(xa_lo, 1)

            def lo_a(a):
                for m in range(KT):
                    dve.wait_ge(a_hi, KT * a + m + 1)
                    dve.tensor_tensor(a_t[:, LO, m, :], (S2, S0)[m][:], f(a_t[:, HI, m, :]), ALU.subtract
                                      ).then_inc(a_lo, 1)

            def tiles(ap):
                return ap.rearrange("p (g n) -> p g n", n=P)

            def soft_max(a):
                dve.wait_ge(score_mm, a + 1)
                if not isinstance(a, int) or a > 0:
                    dve.wait_ge(p_mm, a)
                dve.scalar_tensor_tensor(out=tiles(soft[:]), in0=tiles(S1[:]), scalar=SCALE,
                                         in1=block_mask[:].unsqueeze(1).broadcast_to([P, G, P]),
                                         op0=ALU.mult, op1=ALU.add).then_inc(soft_dve, 1)
                dve.wait_ge(soft_dve, 6 * a + 1)
                dve.tensor_reduce(s_max[:], tiles(soft[:]), AXX, ALU.max).then_inc(soft_dve, 1)
                dve.wait_ge(soft_dve, 6 * a + 2)
                dve.tensor_tensor(tiles(soft[:]), tiles(soft[:]), s_max[:].unsqueeze(2).broadcast_to([P, G, P]),
                                  ALU.subtract).then_inc(soft_dve, 1)

            def soft_norm(a):
                dve.wait_ge(exp_done, a + 1)
                dve.tensor_reduce(s_sum[:], tiles(soft[:]), AXX, ALU.add).then_inc(soft_dve, 1)
                dve.wait_ge(soft_dve, 6 * a + 4)
                dve.reciprocal(s_inv[:], s_sum[:]).then_inc(soft_dve, 1)
                dve.wait_ge(soft_dve, 6 * a + 5)
                dve.tensor_tensor(tiles(soft[:]), tiles(soft[:]), s_inv[:].unsqueeze(2).broadcast_to([P, G, P]),
                                  ALU.mult).then_inc(soft_dve, 1)

            def lo_v(a, n):
                dve.wait_ge(v_hi, 2 * a + n + 1)
                v = v_t[:, :, 2 * n:2 * n + 2, :].rearrange("p s g n -> p s (g n)")
                dve.tensor_tensor(v[:, LO], (S2, S0)[n][:], f(v[:, HI]), ALU.subtract).then_inc(v_lo, 1)

            def lo_p(a):
                dve.wait_ge(p_hi, a + 1)
                dve.tensor_tensor(p_t[:, LO, :], S0[:], f(p_t[:, HI, :]), ALU.subtract).then_inc(p_lo, 1)

            def lo_att(a, blk):
                for m in range(KT):
                    dve.wait_ge(att_hi, KT * a + m + 1)
                    dve.scalar_tensor_tensor(out=att[:, LO, m, :], in0=(S0, S1)[m][:], scalar=bias_col(blk, BP + m),
                                             in1=f(att[:, HI, m, :]), op0=ALU.add, op1=ALU.subtract
                                             ).then_inc(att_lo, 1)

            def split_hidden(j, n):
                dve.wait_ge(gelu_done, TILES * j + n + 1)
                if n >= 3:
                    dve.wait_ge(hid_used, TILES * j + n - 2)
                elif not_first(j):
                    dve.wait_ge(hid_used, TILES * j)
                dve.tensor_copy(hid[:, HI, n % 3, :], gel[:, n % 2, :]).then_inc(hid_hi, 1)
                dve.wait_ge(hid_hi, TILES * j + n + 1)
                dve.tensor_tensor(hid[:, LO, n % 3, :], gel[:, n % 2, :], f(hid[:, HI, n % 3, :]), ALU.subtract
                                  ).then_inc(hid_lo, 1)

            def cms_sum(j, first, blk):
                c = j if first else j - NC
                dve.wait_ge(hid_used, TILES * j + MT)
                if not_first(j):
                    dve.wait_ge(out_sum, KT * j)
                if isinstance(j, int) and j == NC - 1:
                    dve.wait_ge(prep_pe, 8)
                for m in range(KT):
                    dve.scalar_tensor_tensor(out=tok(res[:, m, :]), in0=tok(y_bank[m][:]), scalar=bias_col(blk, CB2 + m),
                                             in1=chunk_bc(one_hot[:, m, :], c), op0=ALU.add, op1=ALU.add
                                             ).then_inc(cms_f, 1)

            def cms_split(j):
                for m in range(KT):
                    dve.wait_ge(cms_hi, KT * j + m + 1)
                    dve.tensor_tensor(cms[:, LO, m, :], res[:, m, :], f(cms[:, HI, m, :]), ALU.subtract
                                      ).then_inc(cms_lo, 1)

            def finish(j, first, blk):
                dve.wait_ge(hid_used, TILES * (j + 1))
                dve.wait_ge(res_done, KT * (j + 1))
                if first or (isinstance(j, int) and j == NC):
                    if not_first(j):
                        dve.wait_ge(mid_stored, 16 * j)
                else:
                    dve.wait_ge(xh_lo, KT * j)
                for m in range(KT):
                    dve.scalar_tensor_tensor(out=x_out[:, m, :], in0=y_bank[m][:], scalar=bias_col(blk, MB2 + m),
                                             in1=res[:, m, :], op0=ALU.add, op1=ALU.add).then_inc(out_sum, 1)
                for m in range(KT):
                    dve.wait_ge(out_sum, KT * j + m + 1)
                    dve.tensor_scalar(x_out[:, m, :], x_out[:, m, :], 0.0, 1.0, ALU.max, ALU.min
                                      ).then_inc(out_clip, 1)

            def slot(j, first):
                a, t, h = side(j, first)
                blk = 0 if first else 1
                startup = isinstance(j, int) and j == -1
                turn = isinstance(j, int) and j == NC - 1
                ablk = 0 if first and not turn else 1
                mlp = has_mlp(j)
                for n in range(TILES):
                    if n == MT:
                        if a is not None:
                            soft_norm(a)
                            lo_v(a, 0)
                        if mlp:
                            cms_sum(j, first, blk)
                            cms_split(j)
                        if a is not None:
                            lo_v(a, 1)
                    if mlp:
                        split_hidden(j, n)
                    if n == 1 and t is not None:
                        if first:
                            tail_gamma(t)
                        else:
                            tail_out(t, (0, 1))
                    if n == 2 and t is not None and not first:
                        tail_out(t, (2, 3))
                    if n == 0 and turn:
                        prep_copy(1, 0, S1)
                        prep_copy(1, 1, S2)
                    if n == 1 and turn:
                        prep_lo(1, 0, S0)
                    if n == 2 and a is not None:
                        lo_att_x(a)
                    if n == 3 and a is not None:
                        lo_a(a)
                    if n == 4 and turn:
                        prep_copy(1, 2, S1)
                    if n == 5 and turn:
                        prep_lo(1, 1, S2)
                    if n == 5 and a is not None:
                        soft_max(a)
                    if n == 8 and h is not None:
                        lo_head_x(h, first)
                    if n == 9 and a is not None:
                        lo_p(a)
                    if h is not None:
                        if n == 10:
                            select(h, first, a)
                        if n == 12:
                            lo_h(h)
                            accumulate(h, first, (0, 1))
                        if n >= 13:
                            accumulate(h, first, (2 * n - 24, 2 * n - 23))
                    if startup and n in (3, 5, 9, 12):
                        for i in {3: range(12, 14), 5: range(14, 16), 9: range(16, 20), 12: range(20, 24)}[n]:
                            lo_piece(i)
                if a is not None:
                    lo_att(a, ablk)
                if h is not None:
                    moments(h)
                if mlp:
                    finish(j, first, blk)
                if h is not None:
                    normalize(h)

            dve.wait_ge(pe_const, 1)
            link(dve.tensor_copy(bias[:], y_bank[0][:, 0:64]))
            lo_head_x(0, True)
            for i in range(4):
                lo_piece(i)
            dve.wait_ge(pe_const, 2)
            link(dve.tensor_copy(g0_sel[:].rearrange("p m b -> p (m b)"), y_bank[1][:, 0:KT * NB]))
            link(dve.tensor_copy(b0_sel[:].rearrange("p m b -> p (m b)"), y_bank[1][:, KT * NB:2 * KT * NB]))
            for to, raw in ((up_bias[0], x_new[:, 1, 0:H]), (up_bias[1], x_new[:, 1, H:2 * H]), (gb3, x_new[:, 0, :])):
                link(dve.tensor_copy(to[0:R, :], raw[0:R, :]))
                link(dve.tensor_copy(to[32:32 + R, :], raw[32:32 + R, :]))
                link(dve.tensor_tensor(to[32:32 + R, :], raw[32:32 + R, :], f(to[32:32 + R, :]), ALU.subtract))
            for i in range(4, 8):
                lo_piece(i)
            select(0, True, None)
            prep_copy(0, 0, hid_bank[0])
            prep_copy(0, 1, hid_bank[1])
            prep_lo(0, 0, hid_bank[2])
            lo_h(0)
            accumulate(0, True, (0, 1, 2, 3))
            prep_copy(0, 2, hid_bank[0])
            accumulate(0, True, (4, 5, 6, 7))
            moments(0)
            prep_lo(0, 1, hid_bank[1])
            normalize(0)
            for i in range(8, 12):
                lo_piece(i)
            run_slots(dve, slot)

        @block.tensor
        def _(pe):
            def mm3(dst, w, v, start, stop):
                pe.matmul(dst, w(HI), v(HI), start=start, stop=False)
                pe.matmul(dst, w(HI), v(LO), start=False, stop=False)
                return pe.matmul(dst, w(LO), v(HI), start=False, stop=stop)

            def cols(i, n=P):
                return slice(i * n, (i + 1) * n)

            def c1(j, n, weights):
                if n == 0:
                    pe.wait_ge(att_lo, KT * (j + 1))
                if n >= 3:
                    pe.wait_ge(gelu_done, TILES * j + n - 2)
                elif not_first(j):
                    pe.wait_ge(gelu_done, TILES * j)
                if weights is not None and n == 0:
                    pe.wait_ge(w_lo, weights + P_C1)
                for k in range(KT):
                    last = mm3(hid_bank[n % 3][:], lambda s: w_c1[:, s, k, cols(n)], lambda s: att[:, s, k, :],
                               k == 0, k == KT - 1)
                last.then_inc(hid_mm, 1)

            def down2(j, n, w):
                pe.wait_ge(hid_lo, TILES * j + n + 1)
                k = n % MT
                for m in range(KT):
                    last = mm3(y_bank[m][:], lambda s: w[:, s, k, cols(m)], lambda s: hid[:, s, n % 3, :],
                               k == 0, k == MT - 1)
                last.then_inc(hid_used, 1)

            def c2(j, n, weights):
                if n == 0 and not_first(j):
                    pe.wait_ge(out_sum, KT * j)
                if n == 0 and weights is not None:
                    pe.wait_ge(w_lo, weights + P_C2)
                down2(j, n, w_c2)

            def m2(j, n, weights):
                if n == 0:
                    pe.wait_ge(cms_f, KT * (j + 1))
                    if weights is not None:
                        pe.wait_ge(w_lo, weights + P_M2)
                down2(j, n + MT, w_m2)

            def m1a(j, n, weights):
                pe.wait_ge(gelu_done, TILES * j + n + MT - 2)
                if n == 0 and weights is not None:
                    pe.wait_ge(w_lo, weights + P_M1)
                for k in range(KT):
                    mm3(hid_bank[(n + MT) % 3][:], lambda s: w_m1[:, s, k, cols(n)], lambda s: att[:, s, k, :],
                        k == 0, False)

            def m1b(j, n):
                if n == 0:
                    pe.wait_ge(cms_lo, KT * (j + 1))
                for k in range(KT):
                    last = mm3(hid_bank[(n + MT) % 3][:], lambda s: w_m1[:, s, KT + k, cols(n)],
                               lambda s: cms[:, s, k, :], False, k == KT - 1)
                last.then_inc(hid_mm, 1)

            def a_proj(a, t, first):
                pe.wait_ge(xa_lo, KT * (a + 1))
                for m in range(KT):
                    if t is not None and not first:
                        pe.wait_ge(gb_add, G * (t - NC) + 2 + m)
                    for k in range(KT):
                        last = mm3((S2, S0)[m][:], lambda s: w_m[:, s, k, cols(m)], lambda s: x_t[:, s, k, :],
                                   k == 0, k == KT - 1)
                    last.then_inc(a_mm, 1)

            def scores(a, t, first):
                pe.wait_ge(a_lo, KT * (a + 1))
                if t is not None and not first:
                    pe.wait_ge(gb_add, G * (t - NC + 1))
                for g in range(G):
                    for k in range(KT):
                        last = mm3(S1[:, cols(g)], lambda s: a_t[:, s, k, cols(g)], lambda s: x_t[:, s, k, cols(g)],
                                   k == 0, k == KT - 1)
                last.then_inc(score_mm, 1)

            def v_proj(a, n):
                if n == 0:
                    pe.wait_ge(a_lo, KT * (a + 1))
                for i in range(2):
                    g = 2 * n + i
                    for k in range(KT):
                        last = mm3((S2, S0)[n][:, cols(i, H)], lambda s: x_t[:, s, k, cols(g)],
                                   lambda s: w_vp[:, s, k, :], k == 0, k == KT - 1)
                last.then_inc(v_mm, 1)

            def p_turn(a):
                pe.wait_ge(soft_dve, 6 * (a + 1))
                pe.wait_ge(v_lo, 2 * (a + 1))
                for g in range(G):
                    last = pe.transpose(S0[:, cols(g)], soft[:, cols(g)], ident[:])
                last.then_inc(p_mm, 1)

            def att_v(a, h):
                pe.wait_ge(p_lo, a + 1)
                for m in range(KT):
                    if h is not None:
                        pe.wait_ge(y_acc, 8 * h + 6 + m)
                    for g in range(G):
                        last = mm3((S0, S1)[m][:, cols(g)], lambda s: v_t[:, s, g, cols(m)],
                                   lambda s: p_t[:, s, cols(g)], True, True)
                    last.then_inc(att_mm, 1)

            def x_turn(h, a):
                pe.wait_ge(x_in, 16 * (h + 1))
                if a is not None:
                    pe.wait_ge(soft_dve, 6 * a + 1)
                for m in range(KT):
                    if m == 1 and a is not None:
                        pe.wait_ge(v_lo, 2 * a + 1)
                    for g in range(G):
                        last = pe.transpose((S1, S2)[m][:, cols(g)], y[:, g, cols(m)], ident[:])
                    last.then_inc(xin_mm, 1)

            def expert_down(h, a, t, first):
                pe.wait_ge(xh_lo, KT * (h + 1))
                for r in range(R):
                    if a is not None:
                        if r == 0:
                            pe.wait_ge(soft_dve, 6 * a + 1)
                        if r == 1:
                            pe.wait_ge(v_lo, 2 * a + 1)
                        if r == 2:
                            pe.wait_ge(p_lo, a + 1)
                    elif not first and r == 0:
                        pe.wait_ge(gb_add, G * (t - NC + 1))
                    for k in range(KT):
                        last = mm3((S1, S2, S0)[r][:], lambda s: e_down[:, s, k, r, :], lambda s: x_t[:, s, k, :],
                                   k == 0, k == KT - 1)
                    last.then_inc(down_mm, 1)

            def expert_up(h, steps, first):
                for u in steps:
                    dst = (S1, S2, S0, S1, S2, S0, S1, S2)[u]
                    if u < 2:
                        pe.wait_ge(sel_dve, 5 * h + 1 + u)
                        if u == 0:
                            pe.wait_ge(masks_done, h + 1)
                    elif u == 2:
                        pe.wait_ge(h_lo, h + 1)
                    else:
                        pe.wait_ge(y_acc, 8 * h + u - 2)
                    for i in range(2):
                        g = 2 * (u % 2) + i
                        if u >= 2:
                            last = mm3(dst[:, cols(i, H)], lambda s: h_t[:, s, cols(g)],
                                       lambda s: e_up[:, s, u // 2 - 1, :], True, True)
                            continue
                        last = pe.matmul(dst[:, cols(i, H)], masks[:, cols(g)], up_bias[0 if first else 1][:],
                                         start=True, stop=first)
                        if not first:
                            for k in range(KT):
                                for s in (HI, LO):
                                    last = pe.matmul(dst[:, i * H + k * P:i * H + (k + 1) * P], x_t[:, s, k, cols(g)],
                                                     ident_r[:], start=False, stop=(k == KT - 1 and s == LO))
                    last.then_inc(up_mm, 1)

            def tail_turn(t):
                for m in range(KT):
                    for g in range(G):
                        if m == 0:
                            pe.wait_ge(y_norm, G * t + g + 1)
                        last = pe.transpose((S1, S2)[m][:, cols(g)], y[:, g, cols(m)], ident[:])
                    last.then_inc(xt_mm, 1)

            def tail_rows(t, gs):
                for g in gs:
                    if g == 0:
                        pe.wait_ge(y_norm, G * (t + 1))
                    if g == 3:
                        pe.wait_ge(gb_add, G * (t - NC) + 1)
                    pe.matmul((S1, S2, S0, S1)[g][:], masks[:, cols(g)], gb3[:], start=True, stop=True
                              ).then_inc(gb_mm, 1)

            def prep_turn(k, n, dst, wait):
                pe.wait_ge(raw_in, 64 * k + wait)
                for d in range(KT):
                    for i in range(KT):
                        last = pe.transpose(dst[:, d * H + i * P:d * H + (i + 1) * P],
                                            x_out[:, n % 2, i * H + d * P:i * H + (d + 1) * P], ident[:])
                return last

            def prep_product(k, n, dst):
                pe.wait_ge(prep_dve, 5 * k + (2, 4)[n])
                right = (res[:, 1, :], x_out[:, 1, :])[n]
                for i in range(KT):
                    for d in range(KT):
                        last = pe.matmul(dst[:, cols(i, H)], res[:, 0, d * H + i * P:d * H + (i + 1) * P],
                                         right[:, cols(d, H)], start=(d == 0), stop=(d == KT - 1))
                last.then_inc(prep_pe, 1)

            def slot(j, first):
                a, t, h = side(j, first)
                mlp = has_mlp(j)
                turn = isinstance(j, int) and j == NC - 1
                weights = (j // NC) * NP if isinstance(j, int) and j in (0, NC) else None
                for n in range(MT):
                    if mlp:
                        c1(j, n, weights)
                        if n >= 2:
                            c2(j, n - 2, weights)
                    if turn and n == 0:
                        prep_turn(1, 0, S1, 32)
                        prep_turn(1, 1, S2, 32).then_inc(prep_pe, 1)
                    if turn and n == 1:
                        prep_product(1, 0, S0)
                    if n == 1 and t is not None:
                        if first:
                            tail_turn(t)
                        else:
                            tail_rows(t, (0, 1))
                    if n == 2 and t is not None and not first:
                        tail_rows(t, (2, 3))
                    if n == 3 and a is not None:
                        if turn:
                            pe.wait_ge(prep_dve, 5 + 3)
                        a_proj(a, t, first)
                    if turn and n == 4:
                        prep_turn(1, 2, S1, 64).then_inc(prep_pe, 1)
                    if turn and n == 5:
                        pe.wait_ge(a_lo, KT * a + 1)
                        prep_product(1, 1, S2)
                    if n == 5 and a is not None:
                        scores(a, t, first)
                if mlp:
                    m1a(j, 0, weights)
                    c2(j, 6, None)
                if a is not None:
                    if turn:
                        pe.wait_ge(prep_dve, 5 + 5)
                    v_proj(a, 0)
                if mlp:
                    m1a(j, 1, None)
                    c2(j, 7, None)
                if a is not None:
                    v_proj(a, 1)
                if mlp:
                    m1a(j, 2, None)
                for n in range(MT):
                    if mlp:
                        if n >= 3:
                            m1a(j, n, None)
                        m1b(j, n)
                        if n >= 2:
                            m2(j, n - 2, weights)
                    if n == 0 and h is not None and first:
                        x_turn(h, a)
                    if n == 1 and a is not None:
                        p_turn(a)
                    if h is not None:
                        if n == 2:
                            expert_down(h, a, t, first)
                        if n == 4:
                            expert_up(h, (0, 1), first)
                        if n >= 5:
                            expert_up(h, (2 * n - 8, 2 * n - 7), first)
                if a is not None:
                    att_v(a, h)
                if mlp:
                    m2(j, 6, None)
                    m2(j, 7, None)

            pe.wait_ge(pool_const, 9 + QB)
            pe.wait_ge(bias_in, 16 * 12)
            pe.transpose(y_bank[0][:, 0:64], gel[0:64, 0, 0:P], ident[0:64, 0:64]).then_inc(pe_const, 1)
            x_turn(0, None)
            pe.wait_ge(rows_in, 16 * 10)
            pe.wait_ge(table_step, TABLES)
            for n in range(2 * KT):
                last = pe.matmul(y_bank[1][:, cols(n)], x_mlp[0:R, 0, cols(n)], mask_r[0:R, :], start=True, stop=True)
            last.then_inc(pe_const, 1)
            pe.wait_ge(w_lo, P_EXP)
            expert_down(0, None, None, True)
            prep_turn(0, 0, hid_bank[0], 32)
            prep_turn(0, 1, hid_bank[1], 32).then_inc(prep_pe, 1)
            prep_product(0, 0, hid_bank[2])
            pe.wait_ge(table_step, TABLES + 3 + 9)
            expert_up(0, (0, 1, 2, 3), True)
            pe.wait_ge(prep_dve, 3)
            prep_turn(0, 2, hid_bank[0], 64).then_inc(prep_pe, 1)
            expert_up(0, (4, 5, 6, 7), True)
            prep_product(0, 1, hid_bank[1])
            pe.wait_ge(prep_dve, 5)
            run_slots(pe, slot)


_INS = ["x", "itok_B_1_2", "itok_B_17_1546"]
_EXPERT = {"W_down": "W_down", "b_down": "b_down", "W_up": "W_up", "b_up": "b_up"}
_L0 = dict(_EXPERT, gamma="gamma", beta="beta")
_L3 = dict(_EXPERT, gamma="ln_w", beta="ln_b")
_ATT = ("Wq", "Wk", "Wv", "Wp", "bp", "cW1", "cb1", "cW2", "cb2", "mW1", "mb1", "mW2", "mb2")


def kernel(**inputs):
    import numpy as _np
    import concourse.bacc as _bacc
    from concourse import mybir as _mybir
    from concourse.bass_utils import run_bass_kernel_spmd as _run

    nc = _bacc.Bacc("TRN2", target_bir_lowering=False, num_devices=1)
    arrays = {}

    def given(name):
        a = _np.ascontiguousarray(inputs[name])
        arrays[f"in_{name}_dram"] = a
        return nc.dram_tensor(f"in_{name}_dram", a.shape, _mybir.dt.from_np(a.dtype), kind="ExternalInput").ap()

    x, role_ids, codes = (given(n) for n in _INS)
    l0 = {k: given(f"L0_cond_{v}") for k, v in _L0.items()}
    l1 = {k: given(f"L1_cond_{k}") for k in _ATT}
    l2 = {k: given(f"L2_cond_{k}") for k in _ATT}
    l3 = {k: given(f"L3_cond_{v}") for k, v in _L3.items()}
    out = nc.dram_tensor("out_0_dram", x.shape, _mybir.dt.float32, kind="ExternalOutput").ap()
    build(nc, x, role_ids, codes, l0, l1, l2, l3, out)
    r = _run(nc, [arrays], core_ids=[0])
    return r.results[0]["out_0_dram"]
```

```python
from contextlib import ExitStack

import concourse.bass as bass
from concourse import mybir

F32 = mybir.dt.float32
F32R = mybir.dt.float32r
I32 = mybir.dt.int32
ALU = mybir.AluOpType
ACT = mybir.ActivationFunctionType
AXX = mybir.AxisListType.X

P = 128
HI, LO = 0, 1
SIDE = (5, 6, 7)
NEG = -3.0e38
EPS = 1e-5


def build(nc, x, role_ids, codes, l0, l1, l2, l3, out):
    NB, S, H = x.shape
    R, _, K = l0["W_down"].shape
    HID = l1["cW1"].shape[1]
    KT = H // P
    MT = HID // P
    T = 512
    G = T // P
    CB = T // S
    NC = NB * S // T
    QB = P // S
    TILES = 2 * MT
    SCALE = float(H) ** -0.5
    assert (K, KT, G, MT, QB) == (P, 2, 4, 8, 4)


    scratch = nc.dram_tensor("x_mid_dram", [NC, P, KT * T], F32, kind="Internal").ap()
    x_rows = x.rearrange("b s h -> (b s) h").rearrange("(c g p) h -> p c g h", g=G, p=P)
    out_rows = out.rearrange("b s h -> (b s) h").rearrange("(c g p) h -> p c g h", g=G, p=P)

    ctx = ExitStack()
    with ctx:
        def sb(name, shape, dt=F32):
            return ctx.enter_context(nc.sbuf_tensor(name, shape, dt))

        def sem(name):
            return ctx.enter_context(nc.semaphore(name))

        w_m = sb("w_m", [P, 2, KT, H], F32R)
        w_vp = sb("w_vp", [P, 2, KT, H], F32R)
        w_c1 = sb("w_c1", [P, 2, KT, HID], F32R)
        w_c2 = sb("w_c2", [P, 2, MT, H], F32R)
        w_m1 = sb("w_m1", [P, 2, 2 * KT, HID], F32R)
        w_m2 = sb("w_m2", [P, 2, MT, H], F32R)
        e_down = sb("e_down", [P, 2, KT, R, K], F32R)
        e_up = sb("e_up", [P, 2, R, H], F32R)
        stage = sb("stage", [P, 4, 512])

        ident = sb("ident", [P, P])
        ident_r = sb("ident_r", [P, P], F32R)
        block_mask = sb("block_mask", [P, P])
        mask_f = sb("mask_f", [P, R, NB])
        mask_r = sb("mask_r", [64, NB])
        mask_t = sb("mask_t", [P, R, NB // QB])
        one_hot = sb("one_hot", [P, KT, NB])
        g0_sel = sb("g0_sel", [P, KT, NB])
        b0_sel = sb("b0_sel", [P, KT, NB])
        bias = sb("bias", [P, 64])
        up_bias = [sb(f"up_bias{i}", [64, H], F32R) for i in range(2)]
        gb3 = sb("gb3", [64, 2 * H], F32R)
        index = sb("index", [P, 4])
        neg_half = sb("neg_half", [P, G])
        present = sb("present", [P, R, NC], I32)

        y = sb("y", [P, G, H])
        x_new = sb("x_new", [P, KT, T])
        x_mlp = sb("x_mlp", [P, KT, T])
        x_out = sb("x_out", [P, KT, T])
        x_t = sb("x_t", [P, 2, KT, T], F32R)
        a_t = sb("a_t", [P, KT, T])
        v_t = sb("v_t", [P, G, H])
        att = sb("att", [P, 2, KT, T], F32R)
        cms = sb("cms", [P, 2, KT, T], F32R)
        res = sb("res", [P, KT, T])
        gel = sb("gel", [P, 2, T])
        hid = sb("hid", [P, 2, 3, T], F32R)
        soft = sb("soft", [P, T])
        sel = sb("sel", [P, T])
        h_t = sb("h_t", [P, 2, T], F32R)
        masks = sb("masks", [64, T], F32R)
        s_max = sb("s_max", [P, G])
        s_sum = sb("s_sum", [P, G])
        s_inv = sb("s_inv", [P, G])
        stats = sb("stats", [P, G, 6])
        mean_var = sb("mean_var", [P, G, 2])
        var_eps = sb("var_eps", [P, G])
        rstd = sb("rstd", [P, G])
        p_t = a_t[:, 0, :]
        sel2 = soft

        bank = [ctx.enter_context(nc.psum_tensor(f"bank{i}", [P, 512], F32)) for i in range(8)]
        hid_bank, y_bank = bank[0:3], bank[3:5]
        S0, S1, S2 = (bank[i] for i in SIDE)

        ids_in, rows_in, bias_in = sem("ids_in"), sem("rows_in"), sem("bias_in")
        stage_in = [sem(f"stage_in{i}") for i in range(4)]
        x_in, mid_in = sem("x_in"), sem("mid_in")
        mid_stored, out_stored = sem("mid_stored"), sem("out_stored")
        pool_const, dve_const, pe_const = sem("pool_const"), sem("dve_const"), sem("pe_const")
        w_hi, w_lo, table_step = sem("w_hi"), sem("w_lo"), sem("table_step")
        prep_pe, prep_act, prep_dve = sem("prep_pe"), sem("prep_act"), sem("prep_dve")
        hid_mm, gelu_done, hid_hi, hid_lo, hid_used = (sem(n) for n in (
            "hid_mm", "gelu_done", "hid_hi", "hid_lo", "hid_used"))
        cms_f, cms_hi, cms_lo, res_done = (sem(n) for n in ("cms_f", "cms_hi", "cms_lo", "res_done"))
        out_sum, out_clip, moved = sem("out_sum"), sem("out_clip"), sem("moved")
        xa_hi, xa_lo, a_mm, a_done = (sem(n) for n in ("xa_hi", "xa_lo", "a_mm", "a_done"))
        v_mm, v_done, score_mm, soft_dve, exp_done = (sem(n) for n in (
            "v_mm", "v_done", "score_mm", "soft_dve", "exp_done"))
        p_mm, p_done, att_mm, att_hi, att_lo = (sem(n) for n in (
            "p_mm", "p_done", "att_mm", "att_hi", "att_lo"))
        xin_mm, xh_hi, xh_lo, down_mm, sel_dve, sel_gelu, h_hi, h_lo = (sem(n) for n in (
            "xin_mm", "xh_hi", "xh_lo", "down_mm", "sel_dve", "sel_gelu", "h_hi", "h_lo"))
        masks_done, up_mm, y_acc, ln_stats, ln_aggr, ln_var, ln_rstd, y_norm = (sem(n) for n in (
            "masks_done", "up_mm", "y_acc", "ln_stats", "ln_aggr", "ln_var", "ln_rstd", "y_norm"))
        xt_mm, x_gamma, x_beta, gb_mm, gb_mul, gb_add = (sem(n) for n in (
            "xt_mm", "x_gamma", "x_beta", "gb_mm", "gb_mul", "gb_add"))

        CB1, MB1, BP, CB2, MB2, BD = 0, MT, 2 * MT, 2 * MT + 2, 2 * MT + 4, 2 * MT + 6

        def bias_col(block, col):
            return bias[:, 32 * block + col:32 * block + col + 1]

        def pieces(expert, layer):
            down = expert["W_down"].rearrange("r (t p) k -> t p r k", p=P)
            up = expert["W_up"].rearrange("r k h -> k r h")
            found = [(down[t], lambda s, t=t: e_down[:, s, t]) for t in range(KT)]
            found += [(up[:, :, P * t:P * t + P], lambda s, t=t: e_up[:, s, :, P * t:P * t + P])
                      for t in range(KT)]

            def wide(w, target):
                rows = w.rearrange("(t p) n -> t p n", p=P)
                return [(rows[t][:, n:n + 512].unsqueeze(1), lambda s, t=t, n=n: target[:, s, t:t + 1, n:n + 512])
                        for t in range(rows.shape[0]) for n in range(0, HID, 512)]

            def narrow(w, target):
                rows = w.rearrange("(t p) n -> p t n", p=P)
                return [(rows[:, t:t + 2, :], lambda s, t=t: target[:, s, t:t + 2, :]) for t in range(0, MT, 2)]

            return (found + wide(layer["cW1"], w_c1) + narrow(layer["cW2"], w_c2)
                    + wide(layer["mW1"], w_m1) + narrow(layer["mW2"], w_m2))

        PIECES = pieces(l0, l1) + pieces(l3, l2)
        NP = len(PIECES) // 2
        P_EXP, P_C1, P_C2, P_M1, P_M2 = 4, 8, 12, 20, 24
        assert NP == P_M2

        TABLES = 5 + R + 1 + KT + 1 + QB * R

        RAWS = 4
        LOADS = NP + RAWS

        def load_of(i):
            return i // NP * LOADS + i % NP + (RAWS if i % NP >= P_EXP else 0)

        def raw_load(k, n):
            return k * LOADS + P_EXP + n

        STARTUP_PIECES = {3: range(4, 7), 5: range(7, 9), 6: range(9, 11), 8: range(11, 14), 9: range(14, 16),
                          11: range(16, 20), 12: range(20, 24)}

        def stage_at(load, src):
            a, b = src.shape[1], src.shape[2]
            return stage[:, load % 4, 0:a * b].rearrange("p (a b) -> p a b", b=b)

        def stage_view(i):
            return stage_at(load_of(i), PIECES[i][0])

        def loaded(eng, load):
            eng.wait_ge(stage_in[load % 4], 16 * (load // 4 + 1))

        def raw(k, n):
            return stage[:, raw_load(k, n) % 4, :]

        def chunk_bc(table, c):
            part = table[:, bass.ds(c * CB, CB)] if not isinstance(c, int) else table[:, c * CB:c * CB + CB]
            return part.unsqueeze(2).broadcast_to([table.shape[0], CB, S])

        def tok(ap):
            return ap.rearrange("p (b s) -> p b s", s=S)

        def f(ap):
            return ap.bitcast(F32)

        def side(j, first):
            if first:
                t = j + 1 if not isinstance(j, int) or j + 1 < NC else None
                h = j + 2 if not isinstance(j, int) or j + 2 < NC else None
                return j + 1, t, h
            a = j + 1 if not isinstance(j, int) or j + 1 < 2 * NC else None
            t = j - 2 if not isinstance(j, int) or j - 2 >= NC else None
            h = j - 1 if not isinstance(j, int) or NC <= j - 1 < 2 * NC else None
            return a, t, h

        def run_slots(eng, slot):
            slot(-1, True)
            slot(0, True)
            with eng.Fori(1, NC - 2) as j:
                slot(j, True)
            slot(NC - 2, True)
            slot(NC - 1, True)
            slot(NC, False)
            slot(NC + 1, False)
            with eng.Fori(NC + 2, 2 * NC - 1) as j:
                slot(j, False)
            for j in range(2 * NC - 1, 2 * NC + 2):
                slot(j, False)

        def has_mlp(j):
            return not isinstance(j, int) or 0 <= j < 2 * NC

        def not_first(j):
            return not isinstance(j, int) or j > 0

        block = ctx.enter_context(nc.Block())

        @block.sync
        def _(sp):
            def wait_place(load):
                if load < 4:
                    return
                k, n = divmod(load - 4, LOADS)
                if P_EXP <= n < P_EXP + RAWS:
                    sp.wait_ge(prep_pe, 4 * k + (1, 1, 3, 4)[n - P_EXP])
                else:
                    sp.wait_ge(w_lo, k * NP + n + 1 - (RAWS if n >= P_EXP else 0))

            def load_piece(i):
                wait_place(load_of(i))
                sp.dma_start(stage_view(i), PIECES[i][0]).then_inc(stage_in[load_of(i) % 4], 16)

            def load_raws(k, layer):
                for n, name in enumerate(("Wq", "Wk", "Wv", "Wp")):
                    load = raw_load(k, n)
                    src = layer[name].rearrange("(t p) n -> p t n", p=P)
                    wait_place(load)
                    sp.dma_start(stage_at(load, src), src).then_inc(stage_in[load % 4], 16)

            def load_x(h):
                if not isinstance(h, int) or h > 0:
                    sp.wait_ge(xt_mm, KT * h)
                c = bass.ds(h, 1)
                sp.dma_start(y[:].unsqueeze(1), x_rows[:, c, :, :]).then_inc(x_in, 16)

            def load_mid(a):
                if isinstance(a, int):
                    sp.wait_ge(mid_stored, 16 * (NC if a > NC + 1 else NC - 1))
                sp.wait_ge(moved, a)
                sp.dma_start(x_new[:].unsqueeze(1), scratch.rearrange("c p (t n) -> p c t n", n=T)[:, bass.ds(a - NC, 1), :, :]
                             ).then_inc(mid_in, 16)

            def store_mid(j):
                sp.wait_ge(out_clip, KT * (j + 1))
                sp.dma_start(scratch.rearrange("c p (t n) -> p c t n", n=T)[:, bass.ds(j, 1), :, :],
                             x_out[:].unsqueeze(1)).then_inc(mid_stored, 16)

            def store_out(t):
                sp.wait_ge(gb_add, G * (t - NC + 1))
                sp.dma_start(out_rows[:, bass.ds(t - NC, 1), :, :], y[:].unsqueeze(1)).then_inc(out_stored, 16)

            load_x(0)
            for i in range(P_EXP):
                load_piece(i)
            load_raws(0, l1)
            for i in range(P_EXP, 9):
                load_piece(i)
            load_x(1)
            for i in range(9, NP):
                load_piece(i)

            def slot(j, first):
                a, t, h = side(j, first)
                if not first and t is not None:
                    store_out(t)
                if first and (not isinstance(j, int) or j + 2 < NC):
                    load_x(j + 2)
                if isinstance(j, int) and j == NC - 1:
                    for i in range(NP + P_EXP, NP + P_C1):
                        load_piece(i)
                    load_mid(NC + 1)
                    for i in range(NP + P_C1, NP + P_M1):
                        load_piece(i)
                    store_mid(NC - 1)
                    for i in range(NP + P_M1, NP + P_M2):
                        load_piece(i)
                    return
                if isinstance(j, int) and j == NC - 2:
                    for i in range(NP, NP + P_EXP):
                        load_piece(i)
                    load_raws(1, l2)
                if first:
                    store_mid(j)
                if isinstance(j, int) and j == NC - 2:
                    load_mid(NC)
                if not first and (not isinstance(j, int) or j + 2 < 2 * NC):
                    load_mid(j + 2)

            slot(0, True)
            with sp.Fori(1, NC - 2) as j:
                slot(j, True)
            slot(NC - 2, True)
            slot(NC - 1, True)
            slot(NC, False)
            slot(NC + 1, False)
            with sp.Fori(NC + 2, 2 * NC - 2) as j:
                slot(j, False)
            for j in range(2 * NC - 2, 2 * NC + 2):
                slot(j, False)
            sp.wait_ge(mid_stored, 16 * NC)
            sp.wait_ge(out_stored, 16 * NC)

        @block.gpsimd
        def _(pool):
            chain = [0]

            def link(ins):
                chain[0] += 1
                ins.then_inc(pool_const, 1)
                pool.wait_ge(pool_const, chain[0])

            link(pool.memset(ident[:], 0.0))
            link(pool.affine_select(out=ident[:], in_=ident[:], compare_op=ALU.not_equal, fill=1.0, base=0,
                                    pattern=[[-1, P]], channel_multiplier=1))
            link(pool.memset(block_mask[:], NEG))
            for q in range(QB):
                link(pool.memset(block_mask[S * q:S * q + S, S * q:S * q + S], 0.0))
            link(pool.memset(neg_half[:], -0.5))
            for t in range(KT):
                link(pool.iota(index[:, t:t + 1], [[0, 1]], base=P * t, channel_multiplier=1,
                               allow_small_or_imprecise_dtypes=True))
            for q in (0, 32):
                link(pool.iota(index[q:q + 32, 2:3], [[0, 1]], base=0, channel_multiplier=1,
                               allow_small_or_imprecise_dtypes=True))
            pool.tensor_copy(ident_r[:], ident[:]).then_inc(pool_const, 1)

            def spread_masks(h, c, before):
                if not isinstance(h, int) or h > 0:
                    pool.wait_ge(up_mm, 8 * h)
                if before is not None:
                    pool.wait_ge(gb_mm, G * (before - NC + 1))
                part = chunk_bc(mask_r, c)
                pool.tensor_tensor(tok(masks[:]), part, part, ALU.mult).then_inc(masks_done, 1)

            def power(h):
                pool.wait_ge(ln_var, h + 1)
                pool.tensor_tensor(rstd[:], var_eps[:], neg_half[:], ALU.pow).then_inc(ln_rstd, 1)

            def add_beta(t):
                for m in range(KT):
                    pool.wait_ge(x_gamma, KT * t + m + 1)
                    pool.tensor_tensor(tok(x_new[:, m, :]), tok(x_new[:, m, :]), chunk_bc(b0_sel[:, m, :], t),
                                       ALU.add).then_inc(x_beta, 1)

            def residual(j):
                pool.wait_ge(moved, j + 1)
                pool.wait_ge(cms_hi, KT * (j + 1))
                for m in range(KT):
                    pool.wait_ge(cms_lo, KT * j + m + 1)
                    pool.tensor_tensor(res[:, m, :], res[:, m, :], x_mlp[:, m, :], ALU.add).then_inc(res_done, 1)

            def split_piece(i):
                src = stage_view(i)
                loaded(pool, load_of(i))
                pool.tensor_copy(PIECES[i][1](HI), src).then_inc(w_hi, 1)
                pool.wait_ge(w_hi, i + 1)
                pool.tensor_tensor(PIECES[i][1](LO), src, f(PIECES[i][1](HI)), ALU.subtract).then_inc(w_lo, 1)

            pool.wait_ge(table_step, TABLES)
            pool.wait_ge(pe_const, 2)
            spread_masks(0, 0, None)
            power(0)

            def slot(j, first):
                a, t, h = side(j, first)
                if first and t is not None:
                    add_beta(t)
                if isinstance(j, int) and j == NC - 2:
                    pool.wait_ge(up_mm, 8 * NC)
                    for i in range(NP, NP + P_EXP):
                        split_piece(i)
                if has_mlp(j):
                    residual(j)
                if h is not None:
                    c = h if first else h - NC
                    spread_masks(h, c, t if not first else None)
                    power(h)
                if isinstance(j, int) and j == NC - 1:
                    pool.wait_ge(hid_used, TILES * j + MT)
                    for i in range(NP + P_EXP, NP + P_C2):
                        split_piece(i)
                    pool.wait_ge(hid_mm, TILES * (j + 1))
                    for i in range(NP + P_C2, NP + P_M1):
                        split_piece(i)
                    pool.wait_ge(hid_used, TILES * (j + 1))
                    for i in range(NP + P_M1, NP + P_M2):
                        split_piece(i)

            run_slots(pool, slot)

        @block.scalar
        def _(act):
            def hi_piece(i):
                loaded(act, load_of(i))
                act.activation(PIECES[i][1](HI), stage_view(i), ACT.Identity).then_inc(w_hi, 1)

            def hi_prep(k, n, src):
                act.wait_ge(prep_pe, 4 * k + (2, 4)[n])
                act.activation((w_m, w_vp)[n][:, HI].rearrange("p t n -> p (t n)"), src[:],
                               ACT.Identity).then_inc(prep_act, 1)

            def hi_head_x(h, first, a):
                if first:
                    for m in range(KT):
                        act.wait_ge(xin_mm, KT * h + m + 1)
                        if a is not None:
                            act.wait_ge(v_mm, 2 * (a + 1))
                        act.activation(x_t[:, HI, m, :], (S1, S2)[m][:], ACT.Identity).then_inc(xh_hi, 1)
                    return
                act.wait_ge(out_clip, KT * (h + 1))
                act.wait_ge(v_mm, 2 * (a + 1) if a is not None else 4 * NC)
                act.wait_ge(up_mm, 8 * h)
                for m in range(KT):
                    act.activation(x_t[:, HI, m, :], x_out[:, m, :], ACT.Identity).then_inc(xh_hi, 1)

            def head_gelu(h):
                act.wait_ge(sel_dve, 5 * (h + 1))
                act.activation(sel[:], sel[:], ACT.Gelu).then_inc(sel_gelu, 1)
                act.wait_ge(sel_gelu, h + 1)
                if not isinstance(h, int) or h > 0:
                    act.wait_ge(up_mm, 8 * h)
                act.activation(h_t[:, HI, :], sel[:], ACT.Identity).then_inc(h_hi, 1)

            def hi_att_x(a, first, h_before):
                if first:
                    act.wait_ge(x_beta, KT * (a + 1))
                else:
                    act.wait_ge(mid_in, 16 * (a - NC + 1))
                if not isinstance(a, int) or a > 0:
                    act.wait_ge(v_mm, 2 * a)
                if h_before is not None:
                    act.wait_ge(up_mm, 8 * h_before + 2)
                for m in range(KT):
                    act.activation(x_t[:, HI, m, :], x_new[:, m, :], ACT.Identity).then_inc(xa_hi, 1)

            def copy_a(a):
                for m in range(KT):
                    act.wait_ge(a_mm, KT * a + m + 1)
                    act.activation(a_t[:, m, :], (S2, S0)[m][:], ACT.Copy).then_inc(a_done, 1)

            def exps(a):
                act.wait_ge(soft_dve, 6 * a + 3)
                act.activation(soft[:], soft[:], ACT.Exp).then_inc(exp_done, 1)

            def copy_v(a, n):
                act.wait_ge(v_mm, 2 * a + n + 1)
                act.activation(v_t[:, 2 * n:2 * n + 2, :].rearrange("p g n -> p (g n)"), (S2, S0)[n][:],
                               ACT.Copy).then_inc(v_done, 1)

            def copy_p(a):
                act.wait_ge(p_mm, a + 1)
                act.activation(p_t[:], S0[:], ACT.Copy).then_inc(p_done, 1)

            def hi_att(a, blk):
                for m in range(KT):
                    act.wait_ge(att_mm, KT * a + m + 1)
                    act.activation(att[:, HI, m, :], (S0, S1)[m][:], ACT.Identity,
                                   bias=bias_col(blk, BP + m)).then_inc(att_hi, 1)

            def gelu(j, n, blk):
                act.wait_ge(hid_mm, TILES * j + n + 1)
                if n >= 2 or not_first(j):
                    act.wait_ge(hid_lo, TILES * j + n - 1)
                col = CB1 + n if n < MT else MB1 + n - MT
                act.activation(gel[:, n % 2, :], hid_bank[n % 3][:], ACT.Gelu,
                               bias=bias_col(blk, col)).then_inc(gelu_done, 1)

            def hi_cms(j):
                for m in range(KT):
                    act.wait_ge(cms_f, KT * j + m + 1)
                    act.activation(cms[:, HI, m, :], res[:, m, :], ACT.Identity).then_inc(cms_hi, 1)

            def move(a):
                if not isinstance(a, int) or a > 0:
                    act.wait_ge(res_done, KT * a)
                act.wait_ge(xa_lo, KT * (a + 1))
                act.activation(x_mlp[:], x_new[:], ACT.Copy).then_inc(moved, 1)

            def slot(j, first):
                a, t, h = side(j, first)
                blk = 0 if first else 1
                ablk = 0 if first and not (isinstance(j, int) and j == NC - 1) else 1
                startup = isinstance(j, int) and j == -1
                turn = isinstance(j, int) and j == NC - 1
                mlp = has_mlp(j)
                h_before = j - 2 if not first and (not isinstance(j, int) or j >= NC + 2) else None
                for n in range(TILES):
                    if n == 3 and a is not None:
                        hi_att_x(a, not ablk, h_before)
                    if n == 12 and h is not None:
                        head_gelu(h)
                    if n == MT and a is not None:
                        exps(a)
                    if n == MT:
                        if mlp:
                            hi_cms(j)
                        if a is not None:
                            copy_v(a, 0)
                            copy_v(a, 1)
                    if mlp:
                        gelu(j, n, blk)
                    if n == 1 and turn:
                        hi_prep(1, 0, S0)
                    if n == 3 and turn:
                        hi_prep(1, 1, S2)
                    if n == 5 and a is not None:
                        copy_a(a)
                    if n == 8 and h is not None:
                        hi_head_x(h, first, a)
                    if n == 9 and a is not None:
                        copy_p(a)
                        move(a)
                    if startup and n in STARTUP_PIECES:
                        for i in STARTUP_PIECES[n]:
                            hi_piece(i)
                if a is not None:
                    hi_att(a, ablk)

            ids = x_mlp[:, 1, :].bitcast(I32)
            act.dma_start(ids[:, 0:NB], role_ids.partition_broadcast(P)).then_inc(ids_in, 16)
            act.dma_start(ids[:, NB:2 * NB], codes.partition_broadcast(P)).then_inc(ids_in, 16)
            act.wait_ge(dve_const, 1)
            for i, (l, e) in enumerate(((l1, l0), (l2, l3))):
                act.dma_start(gel[32 * i + BD:32 * i + BD + R, 0, 0:P], e["b_down"]).then_inc(bias_in, 16)
                for col, name in ((CB1, "cb1"), (MB1, "mb1"), (BP, "bp"), (CB2, "cb2"), (MB2, "mb2")):
                    v = l[name].rearrange("(m p) -> m p", p=P)
                    act.dma_start(gel[32 * i + col:32 * i + col + v.shape[0], 0, 0:P], v).then_inc(bias_in, 16)
            act.dma_start(x_mlp[0:R, 0, 0:H], l0["gamma"]).then_inc(rows_in, 16)
            act.dma_start(x_mlp[0:R, 0, H:2 * H], l0["beta"]).then_inc(rows_in, 16)
            for q in (0, 32):
                act.dma_start(x_new[q:q + R, 0, 0:H], l3["gamma"]).then_inc(rows_in, 16)
                act.dma_start(x_new[q:q + R, 0, H:2 * H], l3["beta"]).then_inc(rows_in, 16)
                act.dma_start(x_new[q:q + R, 1, 0:H], l0["b_up"]).then_inc(rows_in, 16)
                act.dma_start(x_new[q:q + R, 1, H:2 * H], l3["b_up"]).then_inc(rows_in, 16)
            hi_head_x(0, True, None)
            for i in range(P_EXP):
                hi_piece(i)
            hi_prep(0, 0, hid_bank[2])
            head_gelu(0)
            hi_prep(0, 1, hid_bank[1])
            run_slots(act, slot)

        @block.vector
        def _(dve):
            ids = x_mlp[:, 1, :].bitcast(I32)
            work = res
            dve.memset(gel[:, 0, 0:P], 0.0).then_inc(dve_const, 1)
            for r in (*up_bias, gb3):
                last = dve.memset(f(r[:]), 0.0)
            last.then_inc(dve_const, 1)
            chain = [0]

            def link(ins):
                chain[0] += 1
                ins.then_inc(table_step, 1)
                dve.wait_ge(table_step, chain[0])

            dve.wait_ge(ids_in, 32)
            dve.wait_ge(pool_const, 9 + QB)
            roles, code, tmp = work[:, 0, 0:NB], work[:, 0, NB:2 * NB], work[:, 0, 2 * NB:3 * NB]
            link(dve.tensor_copy(roles, ids[:, 0:NB]))
            link(dve.tensor_copy(code, ids[:, NB:2 * NB]))
            link(dve.tensor_scalar(tmp, roles, 0.0, float(R), ALU.is_lt, ALU.mult))
            link(dve.tensor_tensor(roles, roles, tmp, ALU.add))
            link(dve.tensor_scalar(roles, roles, 0.0, float(R - 1), ALU.max, ALU.min))
            for r in range(R):
                link(dve.tensor_scalar(mask_f[:, r, :], roles, float(r), None, ALU.is_equal))
            link(dve.tensor_scalar(mask_r[:], roles[0:64, :], index[0:64, 2:3], None, ALU.is_equal))
            for m in range(KT):
                link(dve.tensor_scalar(one_hot[:, m, :], code, index[:, m:m + 1], None, ALU.is_equal))
            link(dve.tensor_reduce(present[:], mask_f[:].rearrange("p r (c b) -> p r c b", b=CB), AXX, ALU.max))
            for q in range(QB):
                for r in range(R):
                    link(dve.tensor_copy(mask_t[S * q:S * q + S, r, :],
                                         mask_f[S * q:S * q + S, r, :].rearrange("p (g q) -> p q g", q=QB)[:, q, :]))

            def lo_piece(i):
                dve.wait_ge(w_hi, i + 1)
                dve.tensor_tensor(PIECES[i][1](LO), stage_view(i), f(PIECES[i][1](HI)), ALU.subtract).then_inc(w_lo, 1)

            def prep_copy(k, n, src):
                dve.wait_ge(prep_pe, 4 * k + (1, 1, 3)[n])
                dve.tensor_copy(res[:, (0, 1, 0)[n], :], src[:]).then_inc(prep_dve, 1)

            def prep_lo(k, n, src):
                dve.wait_ge(prep_act, 2 * k + n + 1)
                w = (w_m, w_vp)[n]
                dve.tensor_tensor(w[:, LO].rearrange("p t n -> p (t n)"), src[:],
                                  f(w[:, HI].rearrange("p t n -> p (t n)")), ALU.subtract).then_inc(prep_dve, 1)

            def lo_head_x(h, first):
                for m in range(KT):
                    dve.wait_ge(xh_hi, KT * h + m + 1)
                    src = (S1, S2)[m][:] if first else x_out[:, m, :]
                    dve.tensor_tensor(x_t[:, LO, m, :], src, f(x_t[:, HI, m, :]), ALU.subtract).then_inc(xh_lo, 1)

            def select(h, first, a):
                c = h if first else h - NC
                blk = 0 if first else 1
                if a is not None:
                    dve.wait_ge(p_mm, a + 1)
                if not isinstance(h, int) or h > 0:
                    dve.wait_ge(h_lo, h)
                for r in range(R):
                    dve.wait_ge(down_mm, R * h + r + 1)
                    to = (sel, sel2, sel2)[r]
                    if r == 2:
                        dve.wait_ge(sel_dve, 5 * h + 3)
                    dve.scalar_tensor_tensor(out=tok(to[:]), in0=tok((S1, S2, S0)[r][:]), scalar=bias_col(blk, BD + r),
                                             in1=chunk_bc(mask_f[:, r, :], c), op0=ALU.add, op1=ALU.mult
                                             ).then_inc(sel_dve, 1)
                    if r:
                        dve.wait_ge(sel_dve, 5 * h + 2 * r)
                        dve.tensor_tensor(sel[:], sel[:], sel2[:], ALU.add).then_inc(sel_dve, 1)

            def lo_h(h):
                dve.wait_ge(h_hi, h + 1)
                dve.tensor_tensor(h_t[:, LO, :], sel[:], f(h_t[:, HI, :]), ALU.subtract).then_inc(h_lo, 1)

            UP_BANKS = (S1, S2, S0, S1, S2, S0, S1, S2)

            def accumulate(h, first, steps):
                for u in steps:
                    pair = u % 2
                    dve.wait_ge(up_mm, 8 * h + u + 1)
                    src = UP_BANKS[u]
                    yp = y[:, 2 * pair:2 * pair + 2, :].rearrange("p g n -> p (g n)")
                    if u < 2:
                        if first:
                            dve.wait_ge(x_in, 16 * (h + 1))
                            dve.tensor_tensor(yp, src[:], yp, ALU.add).then_inc(y_acc, 1)
                        else:
                            if not isinstance(h, int) or h > NC:
                                dve.wait_ge(out_stored, 16 * (h - NC))
                            dve.tensor_copy(yp, src[:]).then_inc(y_acc, 1)
                        continue
                    dve.wait_ge(y_acc, 8 * h + u - 1)
                    for i in range(2):
                        g = 2 * pair + i
                        c = (h if first else h - NC) * G + g
                        m = mask_t[:, u // 2 - 1, bass.ds(c, 1)]
                        last = dve.scalar_tensor_tensor(out=y[:, g, :], in0=src[:, i * H:(i + 1) * H], scalar=m,
                                                        in1=y[:, g, :], op0=ALU.mult, op1=ALU.add)
                    last.then_inc(y_acc, 1)

            def moments(h):
                for g in range(G):
                    dve.wait_ge(y_acc, 8 * h + 7 + g // 2)
                    dve.bn_stats(stats[:, g, :], y[:, g, :]).then_inc(ln_stats, 1)
                dve.wait_ge(ln_stats, G * (h + 1))
                dve.memset(var_eps[:], 0.0)
                for g in range(G):
                    dve.bn_aggr(mean_var[:, g, :], stats[:, g, :]).then_inc(ln_aggr, 1)
                dve.wait_ge(ln_aggr, G * (h + 1))
                dve.tensor_scalar(var_eps[:], mean_var[:, :, 1], EPS, None, ALU.add).then_inc(ln_var, 1)

            def normalize(h):
                dve.wait_ge(ln_rstd, h + 1)
                for g in range(G):
                    dve.tensor_scalar(y[:, g, :], y[:, g, :], mean_var[:, g, 0:1], rstd[:, g:g + 1],
                                      ALU.subtract, ALU.mult).then_inc(y_norm, 1)

            def tail_gamma(t):
                if not isinstance(t, int) or t > 0:
                    dve.wait_ge(moved, t)
                for m in range(KT):
                    dve.wait_ge(xt_mm, KT * t + m + 1)
                    dve.tensor_tensor(tok(x_new[:, m, :]), tok((S1, S2)[m][:]), chunk_bc(g0_sel[:, m, :], t),
                                      ALU.mult).then_inc(x_gamma, 1)

            def tail_out(t, gs):
                for g in gs:
                    dve.wait_ge(gb_mm, G * (t - NC) + g + 1)
                    src = (S1, S2, S0, S1)[g]
                    dve.tensor_tensor(y[:, g, :], y[:, g, :], src[:, 0:H], ALU.mult).then_inc(gb_mul, 1)
                    dve.wait_ge(gb_mul, G * (t - NC) + g + 1)
                    dve.tensor_tensor(y[:, g, :], y[:, g, :], src[:, H:2 * H], ALU.add).then_inc(gb_add, 1)

            def lo_att_x(a):
                for m in range(KT):
                    dve.wait_ge(xa_hi, KT * a + m + 1)
                    dve.tensor_tensor(x_t[:, LO, m, :], x_new[:, m, :], f(x_t[:, HI, m, :]), ALU.subtract
                                      ).then_inc(xa_lo, 1)

            def tiles(ap):
                return ap.rearrange("p (g n) -> p g n", n=P)

            def soft_max(a):
                dve.wait_ge(score_mm, a + 1)
                if not isinstance(a, int) or a > 0:
                    dve.wait_ge(p_mm, a)
                dve.scalar_tensor_tensor(out=tiles(soft[:]), in0=tiles(S1[:]), scalar=SCALE,
                                         in1=block_mask[:].unsqueeze(1).broadcast_to([P, G, P]),
                                         op0=ALU.mult, op1=ALU.add).then_inc(soft_dve, 1)
                dve.wait_ge(soft_dve, 6 * a + 1)
                dve.tensor_reduce(s_max[:], tiles(soft[:]), AXX, ALU.max).then_inc(soft_dve, 1)
                dve.wait_ge(soft_dve, 6 * a + 2)
                dve.tensor_tensor(tiles(soft[:]), tiles(soft[:]), s_max[:].unsqueeze(2).broadcast_to([P, G, P]),
                                  ALU.subtract).then_inc(soft_dve, 1)

            def soft_norm(a):
                dve.wait_ge(exp_done, a + 1)
                dve.tensor_reduce(s_sum[:], tiles(soft[:]), AXX, ALU.add).then_inc(soft_dve, 1)
                dve.wait_ge(soft_dve, 6 * a + 4)
                dve.reciprocal(s_inv[:], s_sum[:]).then_inc(soft_dve, 1)
                dve.wait_ge(soft_dve, 6 * a + 5)
                dve.tensor_tensor(tiles(soft[:]), tiles(soft[:]), s_inv[:].unsqueeze(2).broadcast_to([P, G, P]),
                                  ALU.mult).then_inc(soft_dve, 1)

            def lo_att(a, blk):
                for m in range(KT):
                    dve.wait_ge(att_hi, KT * a + m + 1)
                    dve.scalar_tensor_tensor(out=att[:, LO, m, :], in0=(S0, S1)[m][:], scalar=bias_col(blk, BP + m),
                                             in1=f(att[:, HI, m, :]), op0=ALU.add, op1=ALU.subtract
                                             ).then_inc(att_lo, 1)

            def split_hidden(j, n):
                dve.wait_ge(gelu_done, TILES * j + n + 1)
                if n >= 3:
                    dve.wait_ge(hid_used, TILES * j + n - 2)
                elif not_first(j):
                    dve.wait_ge(hid_used, TILES * j)
                dve.tensor_copy(hid[:, HI, n % 3, :], gel[:, n % 2, :]).then_inc(hid_hi, 1)
                dve.wait_ge(hid_hi, TILES * j + n + 1)
                dve.tensor_tensor(hid[:, LO, n % 3, :], gel[:, n % 2, :], f(hid[:, HI, n % 3, :]), ALU.subtract
                                  ).then_inc(hid_lo, 1)

            def cms_sum(j, first, blk):
                c = j if first else j - NC
                dve.wait_ge(hid_used, TILES * j + MT)
                if not_first(j):
                    dve.wait_ge(out_sum, KT * j)
                if isinstance(j, int) and j == NC - 1:
                    dve.wait_ge(prep_pe, 8)
                for m in range(KT):
                    dve.scalar_tensor_tensor(out=tok(res[:, m, :]), in0=tok(y_bank[m][:]), scalar=bias_col(blk, CB2 + m),
                                             in1=chunk_bc(one_hot[:, m, :], c), op0=ALU.add, op1=ALU.add
                                             ).then_inc(cms_f, 1)

            def cms_split(j):
                for m in range(KT):
                    dve.wait_ge(cms_hi, KT * j + m + 1)
                    dve.tensor_tensor(cms[:, LO, m, :], res[:, m, :], f(cms[:, HI, m, :]), ALU.subtract
                                      ).then_inc(cms_lo, 1)

            def finish(j, first, blk):
                dve.wait_ge(hid_used, TILES * (j + 1))
                dve.wait_ge(res_done, KT * (j + 1))
                if first or (isinstance(j, int) and j == NC):
                    if not_first(j):
                        dve.wait_ge(mid_stored, 16 * j)
                else:
                    dve.wait_ge(xh_lo, KT * j)
                for m in range(KT):
                    dve.scalar_tensor_tensor(out=x_out[:, m, :], in0=y_bank[m][:], scalar=bias_col(blk, MB2 + m),
                                             in1=res[:, m, :], op0=ALU.add, op1=ALU.add).then_inc(out_sum, 1)
                for m in range(KT):
                    dve.wait_ge(out_sum, KT * j + m + 1)
                    dve.tensor_scalar(x_out[:, m, :], x_out[:, m, :], 0.0, 1.0, ALU.max, ALU.min
                                      ).then_inc(out_clip, 1)

            def slot(j, first):
                a, t, h = side(j, first)
                blk = 0 if first else 1
                startup = isinstance(j, int) and j == -1
                turn = isinstance(j, int) and j == NC - 1
                ablk = 0 if first and not turn else 1
                mlp = has_mlp(j)
                for n in range(TILES):
                    if n == MT:
                        if a is not None:
                            soft_norm(a)
                        if mlp:
                            cms_sum(j, first, blk)
                            cms_split(j)
                    if mlp:
                        split_hidden(j, n)
                    if n == 0 and t is not None:
                        normalize(t)
                    if n == 2 and t is not None:
                        if first:
                            tail_gamma(t)
                        else:
                            tail_out(t, (0, 1))
                    if n == 3 and t is not None and not first:
                        tail_out(t, (2, 3))
                    if n == 0 and turn:
                        prep_copy(1, 0, S1)
                        prep_copy(1, 1, S2)
                    if n == 1 and turn:
                        prep_lo(1, 0, S0)
                    if n == 2 and turn:
                        prep_copy(1, 2, S1)
                    if n == 3 and turn:
                        prep_lo(1, 1, S2)
                    if n == 3 and a is not None:
                        lo_att_x(a)
                    if n == 6 and a is not None:
                        soft_max(a)
                    if n == 8 and h is not None:
                        lo_head_x(h, first)
                    if h is not None:
                        if n == 10:
                            select(h, first, a)
                        if n == 12:
                            lo_h(h)
                            accumulate(h, first, (0, 1))
                        if n >= 13:
                            accumulate(h, first, (2 * n - 24, 2 * n - 23))
                    if startup and n in STARTUP_PIECES:
                        for i in STARTUP_PIECES[n]:
                            lo_piece(i)
                if a is not None:
                    lo_att(a, ablk)
                if h is not None:
                    moments(h)
                if mlp:
                    finish(j, first, blk)

            dve.wait_ge(pe_const, 1)
            link(dve.tensor_copy(bias[:], y_bank[0][:, 0:64]))
            lo_head_x(0, True)
            for i in range(P_EXP):
                lo_piece(i)
            dve.wait_ge(pe_const, 2)
            link(dve.tensor_copy(g0_sel[:].rearrange("p m b -> p (m b)"), y_bank[1][:, 0:KT * NB]))
            link(dve.tensor_copy(b0_sel[:].rearrange("p m b -> p (m b)"), y_bank[1][:, KT * NB:2 * KT * NB]))
            for to, raw in ((up_bias[0], x_new[:, 1, 0:H]), (up_bias[1], x_new[:, 1, H:2 * H]), (gb3, x_new[:, 0, :])):
                link(dve.tensor_copy(to[0:R, :], raw[0:R, :]))
                link(dve.tensor_copy(to[32:32 + R, :], raw[32:32 + R, :]))
                link(dve.tensor_tensor(to[32:32 + R, :], raw[32:32 + R, :], f(to[32:32 + R, :]), ALU.subtract))
            select(0, True, None)
            prep_copy(0, 0, hid_bank[0])
            prep_copy(0, 1, hid_bank[1])
            prep_lo(0, 0, hid_bank[2])
            lo_h(0)
            accumulate(0, True, (0, 1, 2, 3))
            prep_copy(0, 2, hid_bank[0])
            accumulate(0, True, (4, 5, 6, 7))
            moments(0)
            prep_lo(0, 1, hid_bank[1])
            run_slots(dve, slot)

        @block.tensor
        def _(pe):
            def mm3(dst, w, v, start, stop):
                pe.matmul(dst, w(HI), v(HI), start=start, stop=False)
                pe.matmul(dst, w(HI), v(LO), start=False, stop=False)
                return pe.matmul(dst, w(LO), v(HI), start=False, stop=stop)

            def cols(i, n=P):
                return slice(i * n, (i + 1) * n)

            def c1(j, n, weights):
                if n == 0:
                    pe.wait_ge(att_lo, KT * (j + 1))
                if n >= 3:
                    pe.wait_ge(gelu_done, TILES * j + n - 2)
                elif not_first(j):
                    pe.wait_ge(gelu_done, TILES * j)
                if weights is not None and n == 0:
                    pe.wait_ge(w_lo, weights + P_C1)
                for k in range(KT):
                    last = mm3(hid_bank[n % 3][:], lambda s: w_c1[:, s, k, cols(n)], lambda s: att[:, s, k, :],
                               k == 0, k == KT - 1)
                last.then_inc(hid_mm, 1)

            def down2(j, n, w):
                pe.wait_ge(hid_lo, TILES * j + n + 1)
                k = n % MT
                for m in range(KT):
                    last = mm3(y_bank[m][:], lambda s: w[:, s, k, cols(m)], lambda s: hid[:, s, n % 3, :],
                               k == 0, k == MT - 1)
                last.then_inc(hid_used, 1)

            def c2(j, n, weights):
                if n == 0 and not_first(j):
                    pe.wait_ge(out_sum, KT * j)
                if n == 0 and weights is not None:
                    pe.wait_ge(w_lo, weights + P_C2)
                down2(j, n, w_c2)

            def m2(j, n, weights):
                if n == 0:
                    pe.wait_ge(cms_f, KT * (j + 1))
                    if weights is not None:
                        pe.wait_ge(w_lo, weights + P_M2)
                down2(j, n + MT, w_m2)

            def m1a(j, n, weights):
                pe.wait_ge(gelu_done, TILES * j + n + MT - 2)
                if n == 0 and weights is not None:
                    pe.wait_ge(w_lo, weights + P_M1)
                for k in range(KT):
                    mm3(hid_bank[(n + MT) % 3][:], lambda s: w_m1[:, s, k, cols(n)], lambda s: att[:, s, k, :],
                        k == 0, False)

            def m1b(j, n):
                if n == 0:
                    pe.wait_ge(cms_lo, KT * (j + 1))
                for k in range(KT):
                    last = mm3(hid_bank[(n + MT) % 3][:], lambda s: w_m1[:, s, KT + k, cols(n)],
                               lambda s: cms[:, s, k, :], False, k == KT - 1)
                last.then_inc(hid_mm, 1)

            def a_proj(a, t, first):
                pe.wait_ge(xa_lo, KT * (a + 1))
                for m in range(KT):
                    if t is not None and not first:
                        pe.wait_ge(gb_add, G * (t - NC) + 2 + m)
                    for k in range(KT):
                        last = mm3((S2, S0)[m][:], lambda s: w_m[:, s, k, cols(m)], lambda s: x_t[:, s, k, :],
                                   k == 0, k == KT - 1)
                    last.then_inc(a_mm, 1)

            def scores(a, t, first):
                pe.wait_ge(a_done, KT * (a + 1))
                if t is not None and not first:
                    pe.wait_ge(gb_add, G * (t - NC + 1))
                for g in range(G):
                    for k in range(KT):
                        last = pe.matmul(S1[:, cols(g)], a_t[:, k, cols(g)], x_new[:, k, cols(g)],
                                         start=(k == 0), stop=(k == KT - 1))
                last.then_inc(score_mm, 1)

            def v_proj(a, n):
                if n == 0:
                    pe.wait_ge(a_done, KT * (a + 1))
                for i in range(2):
                    g = 2 * n + i
                    for k in range(KT):
                        last = mm3((S2, S0)[n][:, cols(i, H)], lambda s: x_t[:, s, k, cols(g)],
                                   lambda s: w_vp[:, s, k, :], k == 0, k == KT - 1)
                last.then_inc(v_mm, 1)

            def p_turn(a):
                pe.wait_ge(soft_dve, 6 * (a + 1))
                pe.wait_ge(v_done, 2 * (a + 1))
                for g in range(G):
                    last = pe.transpose(S0[:, cols(g)], soft[:, cols(g)], ident[:])
                last.then_inc(p_mm, 1)

            def att_v(a, h):
                pe.wait_ge(p_done, a + 1)
                for m in range(KT):
                    if h is not None:
                        pe.wait_ge(y_acc, 8 * h + 6 + m)
                    for g in range(G):
                        last = pe.matmul((S0, S1)[m][:, cols(g)], v_t[:, g, cols(m)], p_t[:, cols(g)],
                                         start=True, stop=True)
                    last.then_inc(att_mm, 1)

            chosen = [None] * R

            def x_turn(h, a):
                pe.wait_ge(x_in, 16 * (h + 1))
                if a is not None:
                    pe.wait_ge(soft_dve, 6 * a + 1)
                for m in range(KT):
                    if m == 1 and a is not None:
                        pe.wait_ge(v_done, 2 * a + 1)
                    for g in range(G):
                        last = pe.transpose((S1, S2)[m][:, cols(g)], y[:, g, cols(m)], ident[:])
                    last.then_inc(xin_mm, 1)

            def look_up(c):
                for r in range(R):
                    chosen[r] = pe.value_load(present[0:1, r, bass.ds(c, 1)], min_val=0, max_val=1)

            def expert_down(h, a, t, first):
                pe.wait_ge(xh_lo, KT * (h + 1))
                for r in range(R):
                    if a is not None:
                        if r == 0:
                            pe.wait_ge(soft_dve, 6 * a + 1)
                        if r == 1:
                            pe.wait_ge(v_done, 2 * a + 1)
                        if r == 2:
                            pe.wait_ge(p_done, a + 1)
                    elif not first and r == 0:
                        pe.wait_ge(gb_add, G * (t - NC + 1))
                    dst = (S1, S2, S0)[r]
                    with pe.If(chosen[r]):
                        for k in range(KT):
                            last = mm3(dst[:], lambda s: e_down[:, s, k, r, :], lambda s: x_t[:, s, k, :],
                                       k == 0, k == KT - 1)
                        last.then_inc(down_mm, 1)
                    with pe.Else():
                        pe.matmul(dst[:, 0:2], e_down[:, HI, 0, r, :], x_t[:, HI, 0, 0:2], start=True, stop=True
                                  ).then_inc(down_mm, 1)

            def expert_up(h, steps, first):
                for u in steps:
                    dst = (S1, S2, S0, S1, S2, S0, S1, S2)[u]
                    if u < 2:
                        pe.wait_ge(sel_dve, 5 * h + 1 + u)
                        if u == 0:
                            pe.wait_ge(masks_done, h + 1)
                    elif u == 2:
                        pe.wait_ge(h_lo, h + 1)
                    else:
                        pe.wait_ge(y_acc, 8 * h + u - 2)
                    r = u // 2 - 1
                    if u >= 2:
                        with pe.If(chosen[r]):
                            for i in range(2):
                                last = mm3(dst[:, cols(i, H)], lambda s: h_t[:, s, cols(2 * (u % 2) + i)],
                                           lambda s: e_up[:, s, r, :], True, True)
                            last.then_inc(up_mm, 1)
                        with pe.Else():
                            pe.matmul(dst[:, 0:2], h_t[:, HI, cols(0)], e_up[:, HI, r, 0:2], start=True, stop=True
                                      ).then_inc(up_mm, 1)
                        continue
                    for i in range(2):
                        g = 2 * (u % 2) + i
                        last = pe.matmul(dst[:, cols(i, H)], masks[:, cols(g)], up_bias[0 if first else 1][:],
                                         start=True, stop=first)
                        if not first:
                            for k in range(KT):
                                for s in (HI, LO):
                                    last = pe.matmul(dst[:, i * H + k * P:i * H + (k + 1) * P], x_t[:, s, k, cols(g)],
                                                     ident_r[:], start=False, stop=(k == KT - 1 and s == LO))
                    last.then_inc(up_mm, 1)

            def tail_turn(t):
                for m in range(KT):
                    for g in range(G):
                        if m == 0:
                            pe.wait_ge(y_norm, G * t + g + 1)
                        last = pe.transpose((S1, S2)[m][:, cols(g)], y[:, g, cols(m)], ident[:])
                    last.then_inc(xt_mm, 1)

            def tail_rows(t, gs):
                for g in gs:
                    if g == 0:
                        pe.wait_ge(y_norm, G * (t + 1))
                    if g == 3:
                        pe.wait_ge(gb_add, G * (t - NC) + 1)
                    pe.matmul((S1, S2, S0, S1)[g][:], masks[:, cols(g)], gb3[:], start=True, stop=True
                              ).then_inc(gb_mm, 1)

            def prep_turn(k, n, dst):
                loaded(pe, raw_load(k, n))
                for d in range(KT):
                    for i in range(KT):
                        last = pe.transpose(dst[:, d * H + i * P:d * H + (i + 1) * P],
                                            raw(k, n)[:, i * H + d * P:i * H + (d + 1) * P], ident[:])
                return last

            def prep_product(k, n, dst):
                pe.wait_ge(prep_dve, 5 * k + (2, 4)[n])
                if n == 1:
                    loaded(pe, raw_load(k, 3))
                right = (res[:, 1, :], raw(k, 3))[n]
                for i in range(KT):
                    for d in range(KT):
                        last = pe.matmul(dst[:, cols(i, H)], res[:, 0, d * H + i * P:d * H + (i + 1) * P],
                                         right[:, cols(d, H)], start=(d == 0), stop=(d == KT - 1))
                last.then_inc(prep_pe, 1)

            def slot(j, first):
                a, t, h = side(j, first)
                mlp = has_mlp(j)
                turn = isinstance(j, int) and j == NC - 1
                weights = (j // NC) * NP if isinstance(j, int) and j in (0, NC) else None
                for n in range(MT):
                    if mlp:
                        c1(j, n, weights)
                        if n >= 2:
                            c2(j, n - 2, weights)
                    if turn and n == 0:
                        prep_turn(1, 0, S1)
                        prep_turn(1, 1, S2).then_inc(prep_pe, 1)
                    if turn and n == 1:
                        prep_product(1, 0, S0)
                    if turn and n == 2:
                        prep_turn(1, 2, S1).then_inc(prep_pe, 1)
                    if turn and n == 3:
                        prep_product(1, 1, S2)
                    if n == 2 and t is not None:
                        if first:
                            tail_turn(t)
                        else:
                            tail_rows(t, (0, 1))
                    if n == 3 and t is not None and not first:
                        tail_rows(t, (2, 3))
                    if n == 5 and a is not None:
                        if turn:
                            pe.wait_ge(prep_dve, 5 + 5)
                        a_proj(a, t, first)
                    if n == 6 and a is not None:
                        scores(a, t, first)
                if h is not None:
                    look_up(h if first else h - NC)
                if mlp:
                    m1a(j, 0, weights)
                    c2(j, 6, None)
                    c2(j, 7, None)
                if a is not None:
                    v_proj(a, 0)
                if mlp:
                    m1a(j, 1, None)
                if a is not None:
                    v_proj(a, 1)
                if mlp:
                    m1a(j, 2, None)
                for n in range(MT):
                    if mlp:
                        if n >= 3:
                            m1a(j, n, None)
                        m1b(j, n)
                        if n >= 2:
                            m2(j, n - 2, weights)
                    if n == 0 and h is not None and first:
                        x_turn(h, a)
                    if n == 1 and a is not None:
                        p_turn(a)
                    if h is not None:
                        if n == 2:
                            expert_down(h, a, t, first)
                        if n == 4:
                            expert_up(h, (0, 1), first)
                        if n >= 5:
                            expert_up(h, (2 * n - 8, 2 * n - 7), first)
                if a is not None:
                    att_v(a, h)
                if mlp:
                    m2(j, 6, None)
                    m2(j, 7, None)

            pe.wait_ge(pool_const, 9 + QB)
            pe.wait_ge(bias_in, 16 * 12)
            pe.transpose(y_bank[0][:, 0:64], gel[0:64, 0, 0:P], ident[0:64, 0:64]).then_inc(pe_const, 1)
            x_turn(0, None)
            pe.wait_ge(rows_in, 16 * 10)
            pe.wait_ge(table_step, TABLES)
            for n in range(2 * KT):
                last = pe.matmul(y_bank[1][:, cols(n)], x_mlp[0:R, 0, cols(n)], mask_r[0:R, :], start=True, stop=True)
            last.then_inc(pe_const, 1)
            look_up(0)
            pe.wait_ge(w_lo, P_EXP)
            expert_down(0, None, None, True)
            prep_turn(0, 0, hid_bank[0])
            prep_turn(0, 1, hid_bank[1]).then_inc(prep_pe, 1)
            prep_product(0, 0, hid_bank[2])
            pe.wait_ge(table_step, TABLES + 3 + 9)
            expert_up(0, (0, 1, 2, 3), True)
            pe.wait_ge(prep_dve, 3)
            prep_turn(0, 2, hid_bank[0]).then_inc(prep_pe, 1)
            expert_up(0, (4, 5, 6, 7), True)
            prep_product(0, 1, hid_bank[1])
            pe.wait_ge(prep_dve, 5)
            run_slots(pe, slot)


_INS = ["x", "itok_B_1_2", "itok_B_17_1546"]
_EXPERT = {"W_down": "W_down", "b_down": "b_down", "W_up": "W_up", "b_up": "b_up"}
_L0 = dict(_EXPERT, gamma="gamma", beta="beta")
_L3 = dict(_EXPERT, gamma="ln_w", beta="ln_b")
_ATT = ("Wq", "Wk", "Wv", "Wp", "bp", "cW1", "cb1", "cW2", "cb2", "mW1", "mb1", "mW2", "mb2")


def kernel(**inputs):
    import numpy as _np
    import concourse.bacc as _bacc
    from concourse import mybir as _mybir
    from concourse.bass_utils import run_bass_kernel_spmd as _run

    nc = _bacc.Bacc("TRN2", target_bir_lowering=False, num_devices=1)
    arrays = {}

    def given(name):
        a = _np.ascontiguousarray(inputs[name])
        arrays[f"in_{name}_dram"] = a
        return nc.dram_tensor(f"in_{name}_dram", a.shape, _mybir.dt.from_np(a.dtype), kind="ExternalInput").ap()

    x, role_ids, codes = (given(n) for n in _INS)
    l0 = {k: given(f"L0_cond_{v}") for k, v in _L0.items()}
    l1 = {k: given(f"L1_cond_{k}") for k in _ATT}
    l2 = {k: given(f"L2_cond_{k}") for k in _ATT}
    l3 = {k: given(f"L3_cond_{v}") for k, v in _L3.items()}
    out = nc.dram_tensor("out_0_dram", x.shape, _mybir.dt.float32, kind="ExternalOutput").ap()
    build(nc, x, role_ids, codes, l0, l1, l2, l3, out)
    r = _run(nc, [arrays], core_ids=[0])
    return r.results[0]["out_0_dram"]
```

```python
from contextlib import ExitStack

import concourse.bass as bass
from concourse import mybir

F32 = mybir.dt.float32
F32R = mybir.dt.float32r
I32 = mybir.dt.int32
ALU = mybir.AluOpType
ACT = mybir.ActivationFunctionType
AXX = mybir.AxisListType.X

P = 128
HI, LO = 0, 1
SIDE = (5, 6, 7)
NEG = -3.0e38
EPS = 1e-5


def build(nc, x, role_ids, codes, l0, l1, l2, l3, out):
    NB, S, H = x.shape
    R, _, K = l0["W_down"].shape
    HID = l1["cW1"].shape[1]
    KT = H // P
    MT = HID // P
    T = 512
    G = T // P
    CB = T // S
    NC = NB * S // T
    QB = P // S
    TILES = 2 * MT
    SCALE = float(H) ** -0.5
    assert (K, KT, G, MT, QB) == (P, 2, 4, 8, 4)


    x_mid = nc.dram_tensor("x_mid_dram", [NC, P, KT * T], F32, kind="Internal").ap()
    x_mid = x_mid.rearrange("c p (t n) -> p c t n", n=T)
    x_rows = x.rearrange("b s h -> (b s) h")
    out_rows = out.rearrange("b s h -> (b s) h")

    ctx = ExitStack()
    with ctx:
        def sb(name, shape, dt=F32):
            return ctx.enter_context(nc.sbuf_tensor(name, shape, dt))

        def sem(name):
            return ctx.enter_context(nc.semaphore(name))

        w_m = sb("w_m", [P, 2, KT, H], F32R)
        w_vp = sb("w_vp", [P, 2, KT, H], F32R)
        w_c1 = sb("w_c1", [P, 2, KT, HID], F32R)
        w_c2 = sb("w_c2", [P, 2, MT, H], F32R)
        w_m1 = sb("w_m1", [P, 2, 2 * KT, HID], F32R)
        w_m2 = sb("w_m2", [P, 2, MT, H], F32R)
        e_down = sb("e_down", [P, 2, KT, R, K], F32R)
        e_up = sb("e_up", [P, 2, R, H], F32R)
        stage = sb("stage", [P, 4, 512])

        ident = sb("ident", [P, P])
        block_mask = sb("block_mask", [P, P])
        mask_f = sb("mask_f", [P, R, NB])
        mask_r = sb("mask_r", [64, NB])
        mask_t = sb("mask_t", [P, R, NB // QB])
        one_hot = sb("one_hot", [P, KT, NB])
        g0_sel = sb("g0_sel", [P, KT, NB])
        b0_sel = sb("b0_sel", [P, KT, NB])
        bias = sb("bias", [P, 64])
        up_bias = [sb(f"up_bias{i}", [64, H], F32R) for i in range(2)]
        gb3 = sb("gb3", [64, 2 * H], F32R)
        index = sb("index", [P, 3])
        row_no = sb("row_no", [P, NB])
        col_no = sb("col_no", [P, NB])
        rank = sb("rank", [P, 1])
        row_of = sb("row_of", [P, NC * G], I32)
        rows_now = sb("rows_now", [P, G], I32)
        neg_half = sb("neg_half", [P, G])
        idle = sb("idle", [P, G], I32)
        zero = sb("zero", [P, G], I32)
        present = sb("present", [P, R, NC], I32)

        y = sb("y", [P, G, H])
        x_new = sb("x_new", [P, KT, T])
        x_mlp = sb("x_mlp", [P, KT, T])
        x_out = sb("x_out", [P, KT, T])
        x_t = sb("x_t", [P, 2, KT, T], F32R)
        a_t = sb("a_t", [P, KT, T])
        v_t = sb("v_t", [P, G, H])
        att = sb("att", [P, 2, KT, T], F32R)
        cms = sb("cms", [P, 2, KT, T], F32R)
        res = sb("res", [P, KT, T])
        gel = sb("gel", [P, 2, T])
        hid = sb("hid", [P, 2, 3, T], F32R)
        soft = sb("soft", [P, T])
        sel = sb("sel", [P, T])
        h_t = sb("h_t", [P, 2, T], F32R)
        masks = sb("masks", [64, T], F32R)
        s_max = sb("s_max", [P, G])
        s_sum = sb("s_sum", [P, G])
        s_inv = sb("s_inv", [P, G])
        stats = sb("stats", [P, G, 6])
        mean_var = sb("mean_var", [P, G, 2])
        var_eps = sb("var_eps", [P, G])
        rstd = sb("rstd", [P, G])
        p_t = a_t[:, 0, :]
        sel2 = soft

        bank = [ctx.enter_context(nc.psum_tensor(f"bank{i}", [P, 512], F32)) for i in range(8)]
        hid_bank, y_bank = bank[0:3], bank[3:5]
        S0, S1, S2 = (bank[i] for i in SIDE)

        ids_in, rows_in, bias_in = sem("ids_in"), sem("rows_in"), sem("bias_in")
        stage_in = [sem(f"stage_in{i}") for i in range(4)]
        x_in, mid_in = sem("x_in"), sem("mid_in")
        mid_stored, out_stored = sem("mid_stored"), sem("out_stored")
        sort_mm, rows_ready = sem("sort_mm"), sem("rows_ready")
        pool_const, dve_const, pe_const = sem("pool_const"), sem("dve_const"), sem("pe_const")
        w_hi, w_lo, table_step = sem("w_hi"), sem("w_lo"), sem("table_step")
        prep_pe, prep_act, prep_dve = sem("prep_pe"), sem("prep_act"), sem("prep_dve")
        hid_mm, gelu_done, hid_hi, hid_lo, hid_used = (sem(n) for n in (
            "hid_mm", "gelu_done", "hid_hi", "hid_lo", "hid_used"))
        cms_f, cms_hi, cms_lo, res_done = (sem(n) for n in ("cms_f", "cms_hi", "cms_lo", "res_done"))
        out_sum, out_clip, moved = sem("out_sum"), sem("out_clip"), sem("moved")
        xa_hi, xa_lo, a_mm, a_done = (sem(n) for n in ("xa_hi", "xa_lo", "a_mm", "a_done"))
        v_mm, v_done, score_mm, soft_dve, exp_done = (sem(n) for n in (
            "v_mm", "v_done", "score_mm", "soft_dve", "exp_done"))
        p_mm, p_done, att_mm, att_hi, att_lo = (sem(n) for n in (
            "p_mm", "p_done", "att_mm", "att_hi", "att_lo"))
        xin_mm, xh_hi, xh_lo, down_mm, sel_dve, sel_gelu, h_hi, h_lo = (sem(n) for n in (
            "xin_mm", "xh_hi", "xh_lo", "down_mm", "sel_dve", "sel_gelu", "h_hi", "h_lo"))
        masks_done, up_mm, y_acc, ln_stats, ln_aggr, ln_var, ln_rstd, y_norm = (sem(n) for n in (
            "masks_done", "up_mm", "y_acc", "ln_stats", "ln_aggr", "ln_var", "ln_rstd", "y_norm"))
        xt_mm, x_gamma, x_beta, gb_mm, gb_mul, gb_add = (sem(n) for n in (
            "xt_mm", "x_gamma", "x_beta", "gb_mm", "gb_mul", "gb_add"))

        CB1, MB1, BP, CB2, MB2, BD = 0, MT, 2 * MT, 2 * MT + 2, 2 * MT + 4, 2 * MT + 6

        def bias_col(block, col):
            return bias[:, 32 * block + col:32 * block + col + 1]

        def load_bias(eng, i):
            l, e = ((l1, l0), (l2, l3))[i]
            eng.wait_ge(dve_const, 1)
            eng.dma_start(gel[32 * i + BD:32 * i + BD + R, 0, 0:P], e["b_down"]).then_inc(bias_in, 16)
            for col, name in ((CB1, "cb1"), (MB1, "mb1"), (BP, "bp"), (CB2, "cb2"), (MB2, "mb2")):
                v = l[name].rearrange("(m p) -> m p", p=P)
                eng.dma_start(gel[32 * i + col:32 * i + col + v.shape[0], 0, 0:P], v).then_inc(bias_in, 16)

        def pieces(expert, layer):
            down = expert["W_down"].rearrange("r (t p) k -> t p r k", p=P)
            up = expert["W_up"].rearrange("r k h -> k r h")
            found = [(down[t], lambda s, t=t: e_down[:, s, t]) for t in range(KT)]
            found += [(up[:, :, P * t:P * t + P], lambda s, t=t: e_up[:, s, :, P * t:P * t + P])
                      for t in range(KT)]

            def wide(w, target):
                rows = w.rearrange("(t p) n -> t p n", p=P)
                return [(rows[t][:, n:n + 512].unsqueeze(1), lambda s, t=t, n=n: target[:, s, t:t + 1, n:n + 512])
                        for t in range(rows.shape[0]) for n in range(0, HID, 512)]

            def narrow(w, target):
                rows = w.rearrange("(t p) n -> p t n", p=P)
                return [(rows[:, t:t + 2, :], lambda s, t=t: target[:, s, t:t + 2, :]) for t in range(0, MT, 2)]

            return (found + wide(layer["cW1"], w_c1) + narrow(layer["cW2"], w_c2)
                    + wide(layer["mW1"], w_m1) + narrow(layer["mW2"], w_m2))

        PIECES = pieces(l0, l1) + pieces(l3, l2)
        NP = len(PIECES) // 2
        P_EXP, P_C1, P_C2, P_M1, P_M2 = 4, 8, 12, 20, 24
        assert NP == P_M2

        PERM = 5 + 6
        ROWS = PERM + QB
        FLAGS = ROWS + 1 + R + 1
        POOL_TABLES = 7 + QB + KT + QB
        TABLES = FLAGS + 1 + KT + QB * R

        RAWS = 4
        LOADS = NP + RAWS

        def load_of(i):
            return i // NP * LOADS + i % NP + (RAWS if i % NP >= P_EXP else 0)

        def raw_load(k, n):
            return k * LOADS + P_EXP + n

        BY_POOL = P_C2 + 1
        STARTUP_PIECES = {3: range(P_EXP, 7), 5: range(7, 9), 6: range(9, 11), 8: range(11, BY_POOL)}

        def stage_at(load, src):
            a, b = src.shape[1], src.shape[2]
            return stage[:, load % 4, 0:a * b].rearrange("p (a b) -> p a b", b=b)

        def stage_view(i):
            return stage_at(load_of(i), PIECES[i][0])

        def loaded(eng, load):
            eng.wait_ge(stage_in[load % 4], 16 * (load // 4 + 1))

        def raw(k, n):
            return stage[:, raw_load(k, n) % 4, :]

        def chunk_bc(table, c):
            part = table[:, bass.ds(c * CB, CB)] if not isinstance(c, int) else table[:, c * CB:c * CB + CB]
            return part.unsqueeze(2).broadcast_to([table.shape[0], CB, S])

        def tok(ap):
            return ap.rearrange("p (b s) -> p b s", s=S)

        def f(ap):
            return ap.bitcast(F32)

        def side(j, first):
            if first:
                t = j + 1 if not isinstance(j, int) or j + 1 < NC else None
                h = j + 2 if not isinstance(j, int) or j + 2 < NC else None
                return j + 1, t, h
            a = j + 1 if not isinstance(j, int) or j + 1 < 2 * NC else None
            t = j - 2 if not isinstance(j, int) or j - 2 >= NC else None
            h = j - 1 if not isinstance(j, int) or NC <= j - 1 < 2 * NC else None
            return a, t, h

        def run_slots(eng, slot):
            slot(-1, True)
            slot(0, True)
            with eng.Fori(1, NC - 2) as j:
                slot(j, True)
            slot(NC - 2, True)
            slot(NC - 1, True)
            slot(NC, False)
            slot(NC + 1, False)
            with eng.Fori(NC + 2, 2 * NC - 1) as j:
                slot(j, False)
            for j in range(2 * NC - 1, 2 * NC + 2):
                slot(j, False)

        def slot_shift(j):
            return (3, 2) if isinstance(j, int) and j == 0 else (0, 0)

        def has_mlp(j):
            return not isinstance(j, int) or 0 <= j < 2 * NC

        def not_first(j):
            return not isinstance(j, int) or j > 0

        def after_mlps(j):
            return isinstance(j, int) and j >= 2 * NC

        FREE_BANKS = (*hid_bank, y_bank[0])

        def att_banks(a):
            return y_bank if isinstance(a, int) and a == 0 else (S0, S1)

        block = ctx.enter_context(nc.Block())

        @block.sync
        def _(sp):
            def wait_place(load):
                if load < 4:
                    return
                k, n = divmod(load - 4, LOADS)
                if P_EXP <= n < P_EXP + RAWS:
                    sp.wait_ge(prep_pe, 4 * k + (1, 1, 3, 4)[n - P_EXP])
                else:
                    sp.wait_ge(w_lo, k * NP + n + 1 - (RAWS if n >= P_EXP else 0))

            def load_piece(i):
                wait_place(load_of(i))
                sp.dma_start(stage_view(i), PIECES[i][0]).then_inc(stage_in[load_of(i) % 4], 16)

            def load_raws(k, layer):
                for n, name in enumerate(("Wq", "Wk", "Wv", "Wp")):
                    load = raw_load(k, n)
                    src = layer[name].rearrange("(t p) n -> p t n", p=P)
                    wait_place(load)
                    sp.dma_start(stage_at(load, src), src).then_inc(stage_in[load % 4], 16)

            def load_mid(a):
                if isinstance(a, int):
                    sp.wait_ge(mid_stored, 16 * (NC if a > NC + 1 else NC - 1))
                sp.wait_ge(moved, a)
                sp.dma_start(x_new[:].unsqueeze(1), x_mid[:, bass.ds(a - NC, 1), :, :]).then_inc(mid_in, 16)

            def store_mid(j):
                sp.wait_ge(out_clip, KT * (j + 1))
                sp.dma_start(x_mid[:, bass.ds(j, 1), :, :], x_out[:].unsqueeze(1)).then_inc(mid_stored, 16)

            for i in range(P_EXP):
                load_piece(i)
            load_bias(sp, 1)
            for q in (0, 32):
                sp.dma_start(x_new[q:q + R, 0, 0:H], l3["gamma"]).then_inc(rows_in, 16)
                sp.dma_start(x_new[q:q + R, 0, H:2 * H], l3["beta"]).then_inc(rows_in, 16)
                sp.dma_start(x_new[q:q + R, 1, 0:H], l0["b_up"]).then_inc(rows_in, 16)
                sp.dma_start(x_new[q:q + R, 1, H:2 * H], l3["b_up"]).then_inc(rows_in, 16)
            sp.dma_start(x_mlp[0:R, 0, 0:H], l0["gamma"]).then_inc(rows_in, 16)
            sp.dma_start(x_mlp[0:R, 0, H:2 * H], l0["beta"]).then_inc(rows_in, 16)
            load_raws(0, l1)
            for i in range(P_EXP, NP):
                load_piece(i)

            def slot(j, first):
                a, t, h = side(j, first)
                if isinstance(j, int) and j == NC - 1:
                    for i in range(NP + P_EXP, NP + P_C1):
                        load_piece(i)
                    load_mid(NC + 1)
                    for i in range(NP + P_C1, NP + P_M1):
                        load_piece(i)
                    store_mid(NC - 1)
                    for i in range(NP + P_M1, NP + P_M2):
                        load_piece(i)
                    return
                if isinstance(j, int) and j == NC - 2:
                    for i in range(NP, NP + P_EXP):
                        load_piece(i)
                    load_raws(1, l2)
                if first:
                    store_mid(j)
                if isinstance(j, int) and j == NC - 2:
                    load_mid(NC)
                if not first and (not isinstance(j, int) or j + 2 < 2 * NC):
                    load_mid(j + 2)

            slot(0, True)
            with sp.Fori(1, NC - 2) as j:
                slot(j, True)
            slot(NC - 2, True)
            slot(NC - 1, True)
            slot(NC, False)
            slot(NC + 1, False)
            with sp.Fori(NC + 2, 2 * NC - 2) as j:
                slot(j, False)
            for j in range(2 * NC - 2, 2 * NC + 2):
                slot(j, False)
            sp.wait_ge(mid_stored, 16 * NC)
            sp.wait_ge(out_stored, 16 * G * NC)

        @block.gpsimd
        def _(pool):
            chain = [0]

            def link(ins):
                chain[0] += 1
                ins.then_inc(pool_const, 1)
                pool.wait_ge(pool_const, chain[0])

            link(pool.memset(ident[:], 0.0))
            link(pool.affine_select(out=ident[:], in_=ident[:], compare_op=ALU.not_equal, fill=1.0, base=0,
                                    pattern=[[-1, P]], channel_multiplier=1))
            link(pool.memset(block_mask[:], NEG))
            for q in range(QB):
                link(pool.memset(block_mask[S * q:S * q + S, S * q:S * q + S], 0.0))
            link(pool.memset(neg_half[:], -0.5))
            link(pool.memset(zero[:], 0))
            link(pool.iota(row_no[:], [[0, NB]], base=0, channel_multiplier=1, allow_small_or_imprecise_dtypes=True))
            link(pool.iota(col_no[:], [[1, NB]], base=0, channel_multiplier=0, allow_small_or_imprecise_dtypes=True))
            for t in range(KT):
                link(pool.iota(index[:, t:t + 1], [[0, 1]], base=P * t, channel_multiplier=1,
                               allow_small_or_imprecise_dtypes=True))
            for q in range(0, P, 32):
                link(pool.iota(index[q:q + 32, 2:3], [[0, 1]], base=0, channel_multiplier=1,
                               allow_small_or_imprecise_dtypes=True))

            def spread_masks(h, c, before):
                if not isinstance(h, int) or h > 0:
                    pool.wait_ge(up_mm, 8 * h)
                if before is not None:
                    pool.wait_ge(gb_mm, G * (before - NC + 1))
                part = chunk_bc(mask_r, c)
                pool.tensor_tensor(tok(masks[:]), part, part, ALU.mult).then_inc(masks_done, 1)

            def power(h):
                pool.wait_ge(ln_var, h + 1)
                pool.tensor_tensor(rstd[:], var_eps[:], neg_half[:], ALU.pow).then_inc(ln_rstd, 1)

            def add_beta(t):
                for m in range(KT):
                    pool.wait_ge(x_gamma, KT * t + m + 1)
                    pool.tensor_tensor(tok(x_new[:, m, :]), tok(x_new[:, m, :]), chunk_bc(b0_sel[:, m, :], t),
                                       ALU.add).then_inc(x_beta, 1)

            def residual(j):
                pool.wait_ge(moved, j + 1)
                pool.wait_ge(cms_hi, KT * (j + 1))
                for m in range(KT):
                    pool.wait_ge(cms_lo, KT * j + m + 1)
                    pool.tensor_tensor(res[:, m, :], res[:, m, :], x_mlp[:, m, :], ALU.add).then_inc(res_done, 1)

            def split_piece(i):
                src = stage_view(i)
                loaded(pool, load_of(i))
                pool.tensor_copy(PIECES[i][1](HI), src).then_inc(w_hi, 1)
                pool.wait_ge(w_hi, i + 1)
                pool.tensor_tensor(PIECES[i][1](LO), src, f(PIECES[i][1](HI)), ALU.subtract).then_inc(w_lo, 1)

            def take_rows(c, n):
                part = row_of[:, bass.ds(c * G, G)]
                pool.tensor_tensor(rows_now[:], part, zero[:], ALU.add).then_inc(rows_ready, 1)
                pool.wait_ge(rows_ready, n + 1)
                pool.tensor_tensor(idle[:], zero[:], zero[:], ALU.add)

            def load_x(h):
                if not isinstance(h, int) or h > 0:
                    pool.wait_ge(x_in, 16 * G * h)
                    pool.wait_ge(xt_mm, KT * h)
                take_rows(h, h)
                for g in range(G):
                    pool.indirect_dma_start(y[:, g, :], None, x_rows, bass.IndirectOffsetOnAxis(rows_now[:, g:g + 1], 0)
                                            ).then_inc(x_in, 16)

            def store_out(t):
                if isinstance(t, int) and t == NC:
                    pool.wait_ge(x_in, 16 * G * NC)
                else:
                    pool.wait_ge(out_stored, 16 * G * (t - NC))
                last = isinstance(t, int) and t == 2 * NC - 1
                if not last:
                    pool.wait_ge(gb_add, G * (t - NC) + G)
                take_rows(t - NC, t)
                for g in range(G):
                    if last:
                        pool.wait_ge(gb_add, G * (t - NC) + g + 1)
                    pool.indirect_dma_start(out_rows, bass.IndirectOffsetOnAxis(rows_now[:, g:g + 1], 0),
                                            y[:, g, :], None).then_inc(out_stored, 16)

            pool.wait_ge(table_step, ROWS)
            load_x(0)
            pool.wait_ge(table_step, TABLES)
            pool.wait_ge(pe_const, 2)
            spread_masks(0, 0, None)
            power(0)

            def slot(j, first):
                a, t, h = side(j, first)
                if first and t is not None:
                    add_beta(t)
                if first and h is not None:
                    load_x(h)
                last_head = isinstance(j, int) and j == 2 * NC
                if last_head:
                    spread_masks(h, h - NC, t)
                if not first and t is not None:
                    store_out(t)
                if isinstance(j, int) and j == 0:
                    for i in range(P_M1 - 1, P_M2):
                        split_piece(i)
                if isinstance(j, int) and j == NC - 2:
                    pool.wait_ge(up_mm, 8 * NC)
                    for i in range(NP, NP + P_EXP):
                        split_piece(i)
                if has_mlp(j):
                    residual(j)
                if h is not None:
                    c = h if first else h - NC
                    if not last_head:
                        spread_masks(h, c, t if not first else None)
                    startup = isinstance(j, int) and j == -1
                    if startup:
                        pool.wait_ge(w_lo, BY_POOL)
                        for i in range(BY_POOL, P_M1 - 1):
                            split_piece(i)
                    power(h)
                if isinstance(j, int) and j == NC - 1:
                    pool.wait_ge(hid_used, TILES * j + MT)
                    for i in range(NP + P_EXP, NP + P_C2):
                        split_piece(i)
                    pool.wait_ge(hid_mm, TILES * (j + 1))
                    for i in range(NP + P_C2, NP + P_M1):
                        split_piece(i)
                    pool.wait_ge(hid_used, TILES * (j + 1))
                    for i in range(NP + P_M1, NP + P_M2):
                        split_piece(i)

            run_slots(pool, slot)

        @block.scalar
        def _(act):
            def hi_piece(i):
                loaded(act, load_of(i))
                act.activation(PIECES[i][1](HI), stage_view(i), ACT.Identity).then_inc(w_hi, 1)

            def hi_prep(k, n, src):
                act.wait_ge(prep_pe, 4 * k + (2, 4)[n])
                act.activation((w_m, w_vp)[n][:, HI].rearrange("p t n -> p (t n)"), src[:],
                               ACT.Identity).then_inc(prep_act, 1)

            def hi_head_x(h, first, a):
                if first:
                    for m in range(KT):
                        act.wait_ge(xin_mm, KT * h + m + 1)
                        if a is not None:
                            act.wait_ge(v_mm, 2 * (a + 1))
                        act.activation(x_t[:, HI, m, :], (S1, S2)[m][:], ACT.Identity).then_inc(xh_hi, 1)
                    return
                act.wait_ge(out_clip, KT * (h + 1))
                act.wait_ge(v_mm, 2 * (a + 1) if a is not None else 4 * NC)
                act.wait_ge(up_mm, 8 * h)
                for m in range(KT):
                    act.activation(x_t[:, HI, m, :], x_out[:, m, :], ACT.Identity).then_inc(xh_hi, 1)

            def head_gelu(h):
                act.wait_ge(sel_dve, 5 * (h + 1))
                act.activation(sel[:], sel[:], ACT.Gelu).then_inc(sel_gelu, 1)
                act.wait_ge(sel_gelu, h + 1)
                if not isinstance(h, int) or h > 0:
                    act.wait_ge(up_mm, 8 * h)
                act.activation(h_t[:, HI, :], sel[:], ACT.Identity).then_inc(h_hi, 1)

            def hi_att_x(a, first, h_before):
                if first:
                    act.wait_ge(x_beta, KT * (a + 1))
                else:
                    act.wait_ge(mid_in, 16 * (a - NC + 1))
                if not isinstance(a, int) or a > 0:
                    act.wait_ge(v_mm, 2 * a)
                if h_before is not None:
                    act.wait_ge(up_mm, 8 * h_before + 2)
                for m in range(KT):
                    act.activation(x_t[:, HI, m, :], x_new[:, m, :], ACT.Identity).then_inc(xa_hi, 1)

            def copy_a(a):
                for m in range(KT):
                    act.wait_ge(a_mm, KT * a + m + 1)
                    act.activation(a_t[:, m, :], (S2, S0)[m][:], ACT.Copy).then_inc(a_done, 1)

            def exps(a):
                act.wait_ge(soft_dve, 6 * a + 3)
                act.activation(soft[:], soft[:], ACT.Exp).then_inc(exp_done, 1)

            def copy_v(a, n):
                act.wait_ge(v_mm, 2 * a + n + 1)
                act.activation(v_t[:, 2 * n:2 * n + 2, :].rearrange("p g n -> p (g n)"), (S2, S0)[n][:],
                               ACT.Copy).then_inc(v_done, 1)

            def copy_p(a):
                act.wait_ge(p_mm, a + 1)
                act.activation(p_t[:], S0[:], ACT.Copy).then_inc(p_done, 1)

            def hi_att(a, blk):
                for m in range(KT):
                    act.wait_ge(att_mm, KT * a + m + 1)
                    act.activation(att[:, HI, m, :], att_banks(a)[m][:], ACT.Identity,
                                   bias=bias_col(blk, BP + m)).then_inc(att_hi, 1)

            def gelu(j, n, blk):
                act.wait_ge(hid_mm, TILES * j + n + 1)
                if n >= 2 or not_first(j):
                    act.wait_ge(hid_lo, TILES * j + n - 1)
                col = CB1 + n if n < MT else MB1 + n - MT
                act.activation(gel[:, n % 2, :], hid_bank[n % 3][:], ACT.Gelu,
                               bias=bias_col(blk, col)).then_inc(gelu_done, 1)

            def hi_cms(j):
                for m in range(KT):
                    act.wait_ge(cms_f, KT * j + m + 1)
                    act.activation(cms[:, HI, m, :], res[:, m, :], ACT.Identity).then_inc(cms_hi, 1)

            def move(a):
                if not isinstance(a, int) or a > 0:
                    act.wait_ge(res_done, KT * a)
                act.wait_ge(xa_lo, KT * (a + 1))
                act.activation(x_mlp[:], x_new[:], ACT.Copy).then_inc(moved, 1)

            def slot(j, first):
                a, t, h = side(j, first)
                blk = 0 if first else 1
                ablk = 0 if first and not (isinstance(j, int) and j == NC - 1) else 1
                startup = isinstance(j, int) and j == -1
                turn = isinstance(j, int) and j == NC - 1
                mlp = has_mlp(j)
                h_before = j - 2 if not first and (not isinstance(j, int) or j >= NC + 2) else None
                begun, d = slot_shift(j)
                for n in range(TILES):
                    if n == (10 if startup else 12) and h is not None:
                        head_gelu(h)
                    if n == MT and a is not None:
                        exps(a)
                    if n == MT:
                        if mlp:
                            hi_cms(j)
                        if a is not None:
                            copy_v(a, 0)
                            copy_v(a, 1)
                    if mlp and n >= begun:
                        gelu(j, n, blk)
                    if n == 3 + d and a is not None:
                        hi_att_x(a, not ablk, h_before)
                    if n == 1 and turn:
                        hi_prep(1, 0, S0)
                    if n == 3 and turn:
                        hi_prep(1, 1, S2)
                    if n == 5 + d // 2 and a is not None:
                        copy_a(a)
                    if n == 8 and h is not None:
                        hi_head_x(h, first, a)
                    if n == 9 and a is not None:
                        copy_p(a)
                        if startup:
                            hi_att(a, ablk)
                        move(a)
                    if startup and n in STARTUP_PIECES:
                        for i in STARTUP_PIECES[n]:
                            hi_piece(i)
                    if startup and n in (10, 11, 12):
                        gelu(0, n - 10, 0)
                if a is not None and not startup:
                    hi_att(a, ablk)

            ids = x_mlp[:, 1, :].bitcast(I32)
            act.dma_start(ids[:, 0:NB], role_ids.partition_broadcast(P)).then_inc(ids_in, 16)
            act.dma_start(ids[:, NB:2 * NB], codes.partition_broadcast(P)).then_inc(ids_in, 16)
            load_bias(act, 0)
            for i in range(P_EXP):
                hi_piece(i)
            hi_head_x(0, True, None)
            hi_prep(0, 0, hid_bank[2])
            head_gelu(0)
            hi_prep(0, 1, hid_bank[1])
            run_slots(act, slot)

        @block.vector
        def _(dve):
            ids = x_mlp[:, 1, :].bitcast(I32)
            work = x_out
            dve.memset(gel[:, 0, 0:P], 0.0).then_inc(dve_const, 1)
            for r in (*up_bias, gb3):
                last = dve.memset(f(r[:]), 0.0)
            last.then_inc(dve_const, 1)
            chain = [0]

            def link(ins):
                chain[0] += 1
                ins.then_inc(table_step, 1)
                dve.wait_ge(table_step, chain[0])

            dve.wait_ge(ids_in, 32)
            dve.wait_ge(pool_const, POOL_TABLES)
            roles, code, tmp = work[:, 0, 0:NB], work[:, 0, NB:2 * NB], work[:, 0, 2 * NB:3 * NB]
            link(dve.tensor_copy(roles, ids[:, 0:NB]))
            link(dve.tensor_copy(code, ids[:, NB:2 * NB]))
            link(dve.tensor_scalar(tmp, roles, 0.0, float(R), ALU.is_lt, ALU.mult))
            link(dve.tensor_tensor(roles, roles, tmp, ALU.add))
            link(dve.tensor_scalar(roles, roles, 0.0, float(R - 1), ALU.max, ALU.min))
            key, turned = work[:, 0, 3 * NB:4 * NB], work[:, 1, 0:2 * NB]
            key_t, perm = work[:, 1, 2 * NB:3 * NB], work[:, 1, 3 * NB:4 * NB]
            link(dve.scalar_tensor_tensor(out=key, in0=roles, scalar=float(NB), in1=col_no[:],
                                          op0=ALU.mult, op1=ALU.add))
            dve.wait_ge(sort_mm, 1)
            link(dve.scalar_tensor_tensor(out=key_t, in0=y_bank[1][:, 0:NB], scalar=float(NB), in1=row_no[:],
                                          op0=ALU.mult, op1=ALU.add))
            link(dve.tensor_tensor(key, key, key_t, ALU.is_lt))
            link(dve.tensor_reduce(rank[:], key, AXX, ALU.add))
            link(dve.tensor_scalar(perm, col_no[:], rank[:], None, ALU.is_equal))
            link(dve.tensor_copy(turned, y_bank[1][:, 0:2 * NB]))
            dve.wait_ge(sort_mm, 2)
            order = y_bank[0][:, 2 * NB:3 * NB].rearrange("p (g q) -> p q g", q=QB)
            for q in range(QB):
                link(dve.tensor_scalar(row_of[S * q:S * q + S, :], order[S * q:S * q + S, q, :],
                                       float(S), index[S * q:S * q + S, 2:3], ALU.mult, ALU.add))
            link(dve.tensor_copy(work[:, 0, 0:2 * NB], y_bank[0][:, 0:2 * NB]))
            for r in range(R):
                link(dve.tensor_scalar(mask_f[:, r, :], roles, float(r), None, ALU.is_equal))
            link(dve.tensor_reduce(present[:], mask_f[:].rearrange("p r (c b) -> p r c b", b=CB), AXX, ALU.max))

            def lo_piece(i):
                dve.wait_ge(w_hi, i + 1)
                dve.tensor_tensor(PIECES[i][1](LO), stage_view(i), f(PIECES[i][1](HI)), ALU.subtract).then_inc(w_lo, 1)

            def prep_copy(k, n, src):
                dve.wait_ge(prep_pe, 4 * k + (1, 1, 3)[n])
                dve.tensor_copy(res[:, (0, 1, 0)[n], :], src[:]).then_inc(prep_dve, 1)

            def prep_lo(k, n, src):
                dve.wait_ge(prep_act, 2 * k + n + 1)
                w = (w_m, w_vp)[n]
                dve.tensor_tensor(w[:, LO].rearrange("p t n -> p (t n)"), src[:],
                                  f(w[:, HI].rearrange("p t n -> p (t n)")), ALU.subtract).then_inc(prep_dve, 1)

            def lo_head_x(h, first):
                for m in range(KT):
                    dve.wait_ge(xh_hi, KT * h + m + 1)
                    src = (S1, S2)[m][:] if first else x_out[:, m, :]
                    dve.tensor_tensor(x_t[:, LO, m, :], src, f(x_t[:, HI, m, :]), ALU.subtract).then_inc(xh_lo, 1)

            def select(h, first, a):
                c = h if first else h - NC
                blk = 0 if first else 1
                if a is not None:
                    dve.wait_ge(p_mm, a + 1)
                if not isinstance(h, int) or h > 0:
                    dve.wait_ge(h_lo, h)
                for r in range(R):
                    dve.wait_ge(down_mm, R * h + r + 1)
                    to = (sel, sel2, sel2)[r]
                    if r == 2:
                        dve.wait_ge(sel_dve, 5 * h + 3)
                    dve.scalar_tensor_tensor(out=tok(to[:]), in0=tok((S1, S2, S0)[r][:]), scalar=bias_col(blk, BD + r),
                                             in1=chunk_bc(mask_f[:, r, :], c), op0=ALU.add, op1=ALU.mult
                                             ).then_inc(sel_dve, 1)
                    if r:
                        dve.wait_ge(sel_dve, 5 * h + 2 * r)
                        dve.tensor_tensor(sel[:], sel[:], sel2[:], ALU.add).then_inc(sel_dve, 1)

            def lo_h(h):
                dve.wait_ge(h_hi, h + 1)
                dve.tensor_tensor(h_t[:, LO, :], sel[:], f(h_t[:, HI, :]), ALU.subtract).then_inc(h_lo, 1)

            UP_BANKS = (S1, S2, S0, S1, S2, S0, S1, S2)

            def accumulate(h, first, steps):
                for u in steps:
                    pair = u % 2
                    dve.wait_ge(up_mm, 8 * h + u + 1)
                    src = UP_BANKS[u]
                    yp = y[:, 2 * pair:2 * pair + 2, :].rearrange("p g n -> p (g n)")
                    if u < 2:
                        if first:
                            dve.wait_ge(x_in, 16 * G * (h + 1))
                            dve.tensor_tensor(yp, src[:], yp, ALU.add).then_inc(y_acc, 1)
                        else:
                            if not isinstance(h, int) or h > NC:
                                dve.wait_ge(out_stored, 16 * G * (h - NC))
                            dve.tensor_copy(yp, src[:]).then_inc(y_acc, 1)
                        continue
                    dve.wait_ge(y_acc, 8 * h + u - 1)
                    for i in range(2):
                        g = 2 * pair + i
                        c = (h if first else h - NC) * G + g
                        m = mask_t[:, u // 2 - 1, bass.ds(c, 1)]
                        last = dve.scalar_tensor_tensor(out=y[:, g, :], in0=src[:, i * H:(i + 1) * H], scalar=m,
                                                        in1=y[:, g, :], op0=ALU.mult, op1=ALU.add)
                    last.then_inc(y_acc, 1)

            def moments(h):
                for g in range(G):
                    dve.wait_ge(y_acc, 8 * h + 7 + g // 2)
                    dve.bn_stats(stats[:, g, :], y[:, g, :]).then_inc(ln_stats, 1)
                dve.wait_ge(ln_stats, G * (h + 1))
                dve.memset(var_eps[:], 0.0)
                for g in range(G):
                    dve.bn_aggr(mean_var[:, g, :], stats[:, g, :]).then_inc(ln_aggr, 1)
                dve.wait_ge(ln_aggr, G * (h + 1))
                dve.tensor_scalar(var_eps[:], mean_var[:, :, 1], EPS, None, ALU.add).then_inc(ln_var, 1)

            def normalize(h):
                dve.wait_ge(ln_rstd, h + 1)
                for g in range(G):
                    dve.tensor_scalar(y[:, g, :], y[:, g, :], mean_var[:, g, 0:1], rstd[:, g:g + 1],
                                      ALU.subtract, ALU.mult).then_inc(y_norm, 1)

            def tail_gamma(t):
                if not isinstance(t, int) or t > 0:
                    dve.wait_ge(moved, t)
                for m in range(KT):
                    dve.wait_ge(xt_mm, KT * t + m + 1)
                    dve.tensor_tensor(tok(x_new[:, m, :]), tok((S1, S2)[m][:]), chunk_bc(g0_sel[:, m, :], t),
                                      ALU.mult).then_inc(x_gamma, 1)

            def tail_out(t, gs):
                for g in gs:
                    dve.wait_ge(gb_mm, G * (t - NC) + g + 1)
                    dve.wait_ge(y_norm, G * t + g + 1)
                    src = (FREE_BANKS if after_mlps(t + 2) else (S1, S2, S0, S1))[g]
                    dve.tensor_tensor(y[:, g, :], y[:, g, :], src[:, 0:H], ALU.mult).then_inc(gb_mul, 1)
                    dve.wait_ge(gb_mul, G * (t - NC) + g + 1)
                    dve.tensor_tensor(y[:, g, :], y[:, g, :], src[:, H:2 * H], ALU.add).then_inc(gb_add, 1)

            def lo_att_x(a):
                for m in range(KT):
                    dve.wait_ge(xa_hi, KT * a + m + 1)
                    dve.tensor_tensor(x_t[:, LO, m, :], x_new[:, m, :], f(x_t[:, HI, m, :]), ALU.subtract
                                      ).then_inc(xa_lo, 1)

            def tiles(ap):
                return ap.rearrange("p (g n) -> p g n", n=P)

            def soft_max(a):
                dve.wait_ge(score_mm, a + 1)
                if not isinstance(a, int) or a > 0:
                    dve.wait_ge(p_mm, a)
                dve.scalar_tensor_tensor(out=tiles(soft[:]), in0=tiles(S1[:]), scalar=SCALE,
                                         in1=block_mask[:].unsqueeze(1).broadcast_to([P, G, P]),
                                         op0=ALU.mult, op1=ALU.add).then_inc(soft_dve, 1)
                dve.wait_ge(soft_dve, 6 * a + 1)
                dve.tensor_reduce(s_max[:], tiles(soft[:]), AXX, ALU.max).then_inc(soft_dve, 1)
                dve.wait_ge(soft_dve, 6 * a + 2)
                dve.tensor_tensor(tiles(soft[:]), tiles(soft[:]), s_max[:].unsqueeze(2).broadcast_to([P, G, P]),
                                  ALU.subtract).then_inc(soft_dve, 1)

            def soft_norm(a):
                dve.wait_ge(exp_done, a + 1)
                dve.tensor_reduce(s_sum[:], tiles(soft[:]), AXX, ALU.add).then_inc(soft_dve, 1)
                dve.wait_ge(soft_dve, 6 * a + 4)
                dve.reciprocal(s_inv[:], s_sum[:]).then_inc(soft_dve, 1)
                dve.wait_ge(soft_dve, 6 * a + 5)
                dve.tensor_tensor(tiles(soft[:]), tiles(soft[:]), s_inv[:].unsqueeze(2).broadcast_to([P, G, P]),
                                  ALU.mult).then_inc(soft_dve, 1)

            def lo_att(a, blk):
                for m in range(KT):
                    dve.wait_ge(att_hi, KT * a + m + 1)
                    dve.scalar_tensor_tensor(out=att[:, LO, m, :], in0=att_banks(a)[m][:], scalar=bias_col(blk, BP + m),
                                             in1=f(att[:, HI, m, :]), op0=ALU.add, op1=ALU.subtract
                                             ).then_inc(att_lo, 1)

            def split_hidden(j, n):
                dve.wait_ge(gelu_done, TILES * j + n + 1)
                if n >= 3:
                    dve.wait_ge(hid_used, TILES * j + n - 2)
                elif not_first(j):
                    dve.wait_ge(hid_used, TILES * j)
                dve.tensor_copy(hid[:, HI, n % 3, :], gel[:, n % 2, :]).then_inc(hid_hi, 1)
                dve.wait_ge(hid_hi, TILES * j + n + 1)
                dve.tensor_tensor(hid[:, LO, n % 3, :], gel[:, n % 2, :], f(hid[:, HI, n % 3, :]), ALU.subtract
                                  ).then_inc(hid_lo, 1)

            def cms_sum(j, first, blk):
                c = j if first else j - NC
                dve.wait_ge(hid_used, TILES * j + MT)
                if not_first(j):
                    dve.wait_ge(out_sum, KT * j)
                if isinstance(j, int) and j == NC - 1:
                    dve.wait_ge(prep_pe, 8)
                for m in range(KT):
                    dve.scalar_tensor_tensor(out=tok(res[:, m, :]), in0=tok(y_bank[m][:]), scalar=bias_col(blk, CB2 + m),
                                             in1=chunk_bc(one_hot[:, m, :], c), op0=ALU.add, op1=ALU.add
                                             ).then_inc(cms_f, 1)

            def cms_split(j):
                for m in range(KT):
                    dve.wait_ge(cms_hi, KT * j + m + 1)
                    dve.tensor_tensor(cms[:, LO, m, :], res[:, m, :], f(cms[:, HI, m, :]), ALU.subtract
                                      ).then_inc(cms_lo, 1)

            def finish(j, first, blk):
                dve.wait_ge(hid_used, TILES * (j + 1))
                dve.wait_ge(res_done, KT * (j + 1))
                if first or (isinstance(j, int) and j == NC):
                    if not_first(j):
                        dve.wait_ge(mid_stored, 16 * j)
                else:
                    dve.wait_ge(xh_lo, KT * j)
                for m in range(KT):
                    dve.scalar_tensor_tensor(out=x_out[:, m, :], in0=y_bank[m][:], scalar=bias_col(blk, MB2 + m),
                                             in1=res[:, m, :], op0=ALU.add, op1=ALU.add).then_inc(out_sum, 1)

            def clip(j):
                for m in range(KT):
                    dve.wait_ge(out_sum, KT * j + m + 1)
                    dve.tensor_scalar(x_out[:, m, :], x_out[:, m, :], 0.0, 1.0, ALU.max, ALU.min
                                      ).then_inc(out_clip, 1)

            def slot(j, first):
                a, t, h = side(j, first)
                blk = 0 if first else 1
                startup = isinstance(j, int) and j == -1
                turn = isinstance(j, int) and j == NC - 1
                ablk = 0 if first and not turn else 1
                mlp = has_mlp(j)
                last_head = isinstance(j, int) and j == 2 * NC
                begun, d = slot_shift(j)
                for n in range(TILES):
                    if n == MT:
                        if a is not None:
                            soft_norm(a)
                        if mlp:
                            cms_sum(j, first, blk)
                            cms_split(j)
                    if mlp and n >= begun:
                        split_hidden(j, n)
                    if n == 0 and mlp and not_first(j):
                        clip(j - 1)
                    if n == (2 if last_head else d) and t is not None:
                        normalize(t)
                    if n == 2 + d and t is not None:
                        if first:
                            tail_gamma(t)
                        else:
                            tail_out(t, (0, 1))
                    if n == 3 and t is not None and not first:
                        tail_out(t, (2, 3))
                    if n == 0 and turn:
                        prep_copy(1, 0, S1)
                        prep_copy(1, 1, S2)
                    if n == 1 and turn:
                        prep_lo(1, 0, S0)
                    if n == 2 and turn:
                        prep_copy(1, 2, S1)
                    if n == 3 and turn:
                        prep_lo(1, 1, S2)
                    if n == 3 + d and a is not None:
                        lo_att_x(a)
                    if n == 3 and startup:
                        prep_lo(0, 1, hid_bank[1])
                    if n == 6 + d // 2 and a is not None:
                        soft_max(a)
                    if n == (1 if after_mlps(j) else 8) and h is not None:
                        lo_head_x(h, first)
                    if n == 11 and startup:
                        lo_att(a, ablk)
                    if h is not None:
                        if n == 10:
                            select(h, first, a)
                        if n == 12:
                            lo_h(h)
                            accumulate(h, first, (0, 1))
                        if n >= 13:
                            accumulate(h, first, (2 * n - 24, 2 * n - 23))
                    if startup and n in STARTUP_PIECES:
                        for i in STARTUP_PIECES[n]:
                            lo_piece(i)
                    if startup and n in (12, 13, 14):
                        split_hidden(0, n - 12)
                if a is not None and not startup:
                    lo_att(a, ablk)
                last_job = isinstance(j, int) and j == 2 * NC - 1
                if last_job:
                    finish(j, first, blk)
                    clip(j)
                if h is not None:
                    moments(h)
                if mlp and not last_job:
                    finish(j, first, blk)

            for i in range(P_EXP):
                lo_piece(i)
            link(dve.tensor_scalar(mask_r[:], roles[0:64, :], index[0:64, 2:3], None, ALU.is_equal))
            for m in range(KT):
                link(dve.tensor_scalar(one_hot[:, m, :], code, index[:, m:m + 1], None, ALU.is_equal))
            for q in range(QB):
                for r in range(R):
                    link(dve.tensor_copy(mask_t[S * q:S * q + S, r, :],
                                         mask_f[S * q:S * q + S, r, :].rearrange("p (g q) -> p q g", q=QB)[:, q, :]))

            def small_table(to, raw):
                link(dve.tensor_copy(to[0:R, :], raw[0:R, :]))
                link(dve.tensor_copy(to[32:32 + R, :], raw[32:32 + R, :]))
                link(dve.tensor_tensor(to[32:32 + R, :], raw[32:32 + R, :], f(to[32:32 + R, :]), ALU.subtract))

            dve.wait_ge(rows_in, 16 * 10)
            small_table(up_bias[0], x_new[:, 1, 0:H])
            prep_copy(0, 0, hid_bank[0])
            prep_copy(0, 1, hid_bank[1])
            lo_head_x(0, True)
            dve.wait_ge(pe_const, 2)
            link(dve.tensor_copy(bias[:], y_bank[0][:, 0:64]))
            link(dve.tensor_copy(g0_sel[:].rearrange("p m b -> p (m b)"), y_bank[1][:, 0:KT * NB]))
            link(dve.tensor_copy(b0_sel[:].rearrange("p m b -> p (m b)"), y_bank[1][:, KT * NB:2 * KT * NB]))
            small_table(up_bias[1], x_new[:, 1, H:2 * H])
            small_table(gb3, x_new[:, 0, :])
            select(0, True, None)
            prep_lo(0, 0, hid_bank[2])
            lo_h(0)
            accumulate(0, True, (0, 1, 2, 3))
            prep_copy(0, 2, hid_bank[0])
            accumulate(0, True, (4, 5, 6, 7))
            moments(0)
            run_slots(dve, slot)

        @block.tensor
        def _(pe):
            def mm3(dst, w, v, start, stop):
                pe.matmul(dst, w(HI), v(HI), start=start, stop=False)
                pe.matmul(dst, w(HI), v(LO), start=False, stop=False)
                return pe.matmul(dst, w(LO), v(HI), start=False, stop=stop)

            def cols(i, n=P):
                return slice(i * n, (i + 1) * n)

            def c1(j, n, weights):
                if n == 0:
                    pe.wait_ge(att_lo, KT * (j + 1))
                if n >= 3:
                    pe.wait_ge(gelu_done, TILES * j + n - 2)
                elif not_first(j):
                    pe.wait_ge(gelu_done, TILES * j)
                if weights is not None and n == 0:
                    pe.wait_ge(w_lo, weights + P_C1)
                for k in range(KT):
                    last = mm3(hid_bank[n % 3][:], lambda s: w_c1[:, s, k, cols(n)], lambda s: att[:, s, k, :],
                               k == 0, k == KT - 1)
                last.then_inc(hid_mm, 1)

            def down2(j, n, w):
                pe.wait_ge(hid_lo, TILES * j + n + 1)
                k = n % MT
                for m in range(KT):
                    last = mm3(y_bank[m][:], lambda s: w[:, s, k, cols(m)], lambda s: hid[:, s, n % 3, :],
                               k == 0, k == MT - 1)
                last.then_inc(hid_used, 1)

            def c2(j, n, weights):
                if n == 0 and not_first(j):
                    pe.wait_ge(out_sum, KT * j)
                if n == 0 and weights is not None:
                    pe.wait_ge(w_lo, weights + P_C2)
                down2(j, n, w_c2)

            def m2(j, n, weights):
                if n == 0:
                    pe.wait_ge(cms_f, KT * (j + 1))
                    if weights is not None:
                        pe.wait_ge(w_lo, weights + P_M2)
                down2(j, n + MT, w_m2)

            def m1a(j, n, weights):
                pe.wait_ge(gelu_done, TILES * j + n + MT - 2)
                if n == 0 and weights is not None:
                    pe.wait_ge(w_lo, weights + P_M1)
                for k in range(KT):
                    mm3(hid_bank[(n + MT) % 3][:], lambda s: w_m1[:, s, k, cols(n)], lambda s: att[:, s, k, :],
                        k == 0, False)

            def m1b(j, n):
                if n == 0:
                    pe.wait_ge(cms_lo, KT * (j + 1))
                for k in range(KT):
                    last = mm3(hid_bank[(n + MT) % 3][:], lambda s: w_m1[:, s, KT + k, cols(n)],
                               lambda s: cms[:, s, k, :], False, k == KT - 1)
                last.then_inc(hid_mm, 1)

            def a_proj(a, t, first):
                pe.wait_ge(xa_lo, KT * (a + 1))
                for m in range(KT):
                    if t is not None and not first:
                        pe.wait_ge(gb_add, G * (t - NC) + 2 + m)
                    for k in range(KT):
                        last = mm3((S2, S0)[m][:], lambda s: w_m[:, s, k, cols(m)], lambda s: x_t[:, s, k, :],
                                   k == 0, k == KT - 1)
                    last.then_inc(a_mm, 1)

            def scores(a, t, first):
                pe.wait_ge(a_done, KT * (a + 1))
                if t is not None and not first:
                    pe.wait_ge(gb_add, G * (t - NC + 1))
                for g in range(G):
                    for k in range(KT):
                        last = pe.matmul(S1[:, cols(g)], a_t[:, k, cols(g)], x_new[:, k, cols(g)],
                                         start=(k == 0), stop=(k == KT - 1))
                last.then_inc(score_mm, 1)

            def v_proj(a, n):
                if n == 0:
                    pe.wait_ge(a_done, KT * (a + 1))
                for i in range(2):
                    g = 2 * n + i
                    for k in range(KT):
                        last = mm3((S2, S0)[n][:, cols(i, H)], lambda s: x_t[:, s, k, cols(g)],
                                   lambda s: w_vp[:, s, k, :], k == 0, k == KT - 1)
                last.then_inc(v_mm, 1)

            def p_turn(a):
                pe.wait_ge(soft_dve, 6 * (a + 1))
                pe.wait_ge(v_done, 2 * (a + 1))
                for g in range(G):
                    last = pe.transpose(S0[:, cols(g)], soft[:, cols(g)], ident[:])
                last.then_inc(p_mm, 1)

            def att_v(a, h):
                pe.wait_ge(p_done, a + 1)
                for m in range(KT):
                    if h is not None:
                        pe.wait_ge(y_acc, 8 * h + 6 + m)
                    for g in range(G):
                        last = pe.matmul(att_banks(a)[m][:, cols(g)], v_t[:, g, cols(m)], p_t[:, cols(g)],
                                         start=True, stop=True)
                    last.then_inc(att_mm, 1)

            chosen = [None] * R

            def x_turn(h, a):
                pe.wait_ge(x_in, 16 * G * (h + 1))
                if a is not None:
                    pe.wait_ge(soft_dve, 6 * a + 1)
                for m in range(KT):
                    if m == 1 and a is not None:
                        pe.wait_ge(v_done, 2 * a + 1)
                    for g in range(G):
                        last = pe.transpose((S1, S2)[m][:, cols(g)], y[:, g, cols(m)], ident[:])
                    last.then_inc(xin_mm, 1)

            def look_up(c):
                for r in range(R):
                    chosen[r] = pe.value_load(present[0:1, r, bass.ds(c, 1)], min_val=0, max_val=1)

            def expert_down(h, a, t, first):
                pe.wait_ge(xh_lo, KT * (h + 1))
                for r in range(R):
                    if a is not None:
                        if r == 0:
                            pe.wait_ge(soft_dve, 6 * a + 1)
                        if r == 1:
                            pe.wait_ge(v_done, 2 * a + 1)
                        if r == 2:
                            pe.wait_ge(p_done, a + 1)
                    elif not first and r == 0:
                        pe.wait_ge(y_acc, 8 * h)
                    dst = (S1, S2, S0)[r]
                    with pe.If(chosen[r]):
                        for k in range(KT):
                            last = mm3(dst[:], lambda s: e_down[:, s, k, r, :], lambda s: x_t[:, s, k, :],
                                       k == 0, k == KT - 1)
                        last.then_inc(down_mm, 1)
                    with pe.Else():
                        pe.matmul(dst[:, 0:2], e_down[:, HI, 0, r, :], x_t[:, HI, 0, 0:2], start=True, stop=True
                                  ).then_inc(down_mm, 1)

            def expert_up(h, steps, first):
                for u in steps:
                    dst = (S1, S2, S0, S1, S2, S0, S1, S2)[u]
                    if u < 2:
                        pe.wait_ge(sel_dve, 5 * h + 1 + u)
                    elif u == 2:
                        pe.wait_ge(h_lo, h + 1)
                    else:
                        pe.wait_ge(y_acc, 8 * h + u - 2)
                    if u == (0 if first else 2):
                        pe.wait_ge(masks_done, h + 1)
                    r = u // 2 - 1
                    if u >= 2:
                        with pe.If(chosen[r]):
                            for i in range(2):
                                g = 2 * (u % 2) + i
                                if not first:
                                    pe.matmul(dst[:, cols(i, H)], masks[:, cols(g)], up_bias[1][:],
                                              start=True, stop=False)
                                last = mm3(dst[:, cols(i, H)], lambda s: h_t[:, s, cols(g)],
                                           lambda s: e_up[:, s, r, :], first, True)
                            last.then_inc(up_mm, 1)
                        with pe.Else():
                            pe.matmul(dst[:, 0:2], h_t[:, HI, cols(0)], e_up[:, HI, r, 0:2], start=True, stop=True
                                      ).then_inc(up_mm, 1)
                        continue
                    for i in range(2):
                        g = 2 * (u % 2) + i
                        if first:
                            last = pe.matmul(dst[:, cols(i, H)], masks[:, cols(g)], up_bias[0][:],
                                             start=True, stop=True)
                        else:
                            for k in range(KT):
                                last = pe.transpose(dst[:, i * H + k * P:i * H + (k + 1) * P], x_out[:, k, cols(g)],
                                                    ident[:])
                    last.then_inc(up_mm, 1)

            def tail_turn(t):
                for m in range(KT):
                    for g in range(G):
                        if m == 0:
                            pe.wait_ge(y_norm, G * t + g + 1)
                        last = pe.transpose((S1, S2)[m][:, cols(g)], y[:, g, cols(m)], ident[:])
                    last.then_inc(xt_mm, 1)

            def tail_rows(t, gs):
                free = after_mlps(t + 2)
                for g in gs:
                    if free:
                        if g == 0 and t == 2 * NC - 1:
                            pe.wait_ge(gb_add, G * (t - NC))
                        if g == 3 and t == 2 * NC - 2:
                            pe.wait_ge(out_sum, KT * 2 * NC)
                    elif g == 0:
                        pe.wait_ge(y_acc, 8 * (t + 1))
                    elif g == 3:
                        pe.wait_ge(gb_add, G * (t - NC) + 1)
                    pe.matmul((FREE_BANKS if free else (S1, S2, S0, S1))[g][:], masks[:, cols(g)], gb3[:],
                              start=True, stop=True).then_inc(gb_mm, 1)

            def prep_turn(k, n, dst):
                loaded(pe, raw_load(k, n))
                for d in range(KT):
                    for i in range(KT):
                        last = pe.transpose(dst[:, d * H + i * P:d * H + (i + 1) * P],
                                            raw(k, n)[:, i * H + d * P:i * H + (d + 1) * P], ident[:])
                return last

            def prep_product(k, n, dst):
                pe.wait_ge(prep_dve, 5 * k + (2, 4)[n])
                if n == 1:
                    loaded(pe, raw_load(k, 3))
                right = (res[:, 1, :], raw(k, 3))[n]
                for i in range(KT):
                    for d in range(KT):
                        last = pe.matmul(dst[:, cols(i, H)], res[:, 0, d * H + i * P:d * H + (i + 1) * P],
                                         right[:, cols(d, H)], start=(d == 0), stop=(d == KT - 1))
                last.then_inc(prep_pe, 1)

            def slot(j, first):
                a, t, h = side(j, first)
                mlp = has_mlp(j)
                turn = isinstance(j, int) and j == NC - 1
                startup = isinstance(j, int) and j == -1
                begun, d = slot_shift(j)
                last_head = isinstance(j, int) and j == 2 * NC
                ups = (2, 4, 5, 6) if startup else (4, 5, 6, 7)
                weights = (j // NC) * NP if isinstance(j, int) and j in (0, NC) else None
                for n in range(MT):
                    if mlp:
                        if n >= begun:
                            c1(j, n, weights)
                        if n >= max(2, begun):
                            c2(j, n - 2, weights)
                    if turn and n == 0:
                        prep_turn(1, 0, S1)
                        prep_turn(1, 1, S2).then_inc(prep_pe, 1)
                    if turn and n == 1:
                        prep_product(1, 0, S0)
                    if turn and n == 2:
                        prep_turn(1, 2, S1).then_inc(prep_pe, 1)
                    if turn and n == 3:
                        prep_product(1, 1, S2)
                    if n == 1 and last_head:
                        tail_rows(t, range(G))
                        look_up(h - NC)
                        expert_down(h, a, t, first)
                    if n == 2 + d and t is not None and not last_head:
                        if first:
                            tail_turn(t)
                        else:
                            tail_rows(t, (0, 1))
                    if n == 3 and t is not None and not first and not last_head:
                        tail_rows(t, (2, 3))
                    if n == 5 + d // 2 and a is not None:
                        if turn:
                            pe.wait_ge(prep_dve, 5 + 5)
                        if startup:
                            pe.wait_ge(prep_dve, 3)
                        a_proj(a, t, first)
                    if n == 6 + d // 2 and a is not None:
                        scores(a, t, first)
                if h is not None and not last_head:
                    look_up(h if first else h - NC)
                if mlp:
                    m1a(j, 0, weights)
                    c2(j, 6, None)
                    c2(j, 7, None)
                if startup:
                    pe.wait_ge(prep_dve, 5)
                if a is not None:
                    v_proj(a, 0)
                if mlp:
                    m1a(j, 1, None)
                if a is not None:
                    v_proj(a, 1)
                if mlp:
                    m1a(j, 2, None)
                for n in range(MT):
                    if mlp:
                        if n >= 3:
                            m1a(j, n, None)
                        m1b(j, n)
                        if n >= 2:
                            m2(j, n - 2, weights)
                    if n == 0 and h is not None and first:
                        x_turn(h, a)
                    if n == 1 and a is not None:
                        p_turn(a)
                    if h is not None:
                        if n == 2 and not last_head:
                            expert_down(h, a, t, first)
                            if startup:
                                att_v(a, None)
                        if n in ups:
                            expert_up(h, (2 * ups.index(n), 2 * ups.index(n) + 1), first)
                    if startup and n in (2, 3, 4):
                        c1(0, n - 2, 0)
                    if startup and n == 4:
                        c2(0, 0, 0)
                if a is not None and not startup:
                    att_v(a, h)
                if mlp:
                    m2(j, 6, None)
                    m2(j, 7, None)

            pe.wait_ge(pool_const, POOL_TABLES)
            ids_f = x_out[:, 0, 0:2 * NB]
            pe.wait_ge(table_step, 5)
            for i in range(2):
                last = pe.transpose(y_bank[1][:, cols(i, NB)], ids_f[:, cols(i, NB)], ident[:])
            last.then_inc(sort_mm, 1)
            for g in range(G):
                pe.transpose(S0[:, cols(g)], ident[:], ident[:])
            pe.wait_ge(table_step, PERM)
            for i, left in enumerate((x_out[:, 1, 0:NB], x_out[:, 1, NB:2 * NB], row_no[:])):
                last = pe.matmul(y_bank[0][:, cols(i, NB)], left, x_out[:, 1, 3 * NB:4 * NB], start=True, stop=True)
            last.then_inc(sort_mm, 1)
            pe.wait_ge(table_step, FLAGS)
            pe.wait_ge(bias_in, 16 * 12)
            pe.transpose(y_bank[0][:, 0:64], gel[0:64, 0, 0:P], ident[0:64, 0:64]).then_inc(pe_const, 1)
            look_up(0)
            prep_turn(0, 0, hid_bank[0])
            prep_turn(0, 1, hid_bank[1]).then_inc(prep_pe, 1)
            x_turn(0, None)
            pe.wait_ge(rows_in, 16 * 10)
            pe.wait_ge(table_step, TABLES)
            for n in range(2 * KT):
                last = pe.matmul(y_bank[1][:, cols(n)], x_mlp[0:R, 0, cols(n)], mask_r[0:R, :], start=True, stop=True)
            last.then_inc(pe_const, 1)
            pe.wait_ge(w_lo, P_EXP)
            expert_down(0, None, None, True)
            prep_product(0, 0, hid_bank[2])
            pe.wait_ge(table_step, TABLES + 3)
            expert_up(0, (0, 1), True)
            prep_turn(0, 2, hid_bank[0]).then_inc(prep_pe, 1)
            expert_up(0, (2, 3), True)
            expert_up(0, (4, 5, 6, 7), True)
            prep_product(0, 1, hid_bank[1])
            run_slots(pe, slot)


_INS = ["x", "itok_B_1_2", "itok_B_17_1546"]
_EXPERT = {"W_down": "W_down", "b_down": "b_down", "W_up": "W_up", "b_up": "b_up"}
_L0 = dict(_EXPERT, gamma="gamma", beta="beta")
_L3 = dict(_EXPERT, gamma="ln_w", beta="ln_b")
_ATT = ("Wq", "Wk", "Wv", "Wp", "bp", "cW1", "cb1", "cW2", "cb2", "mW1", "mb1", "mW2", "mb2")


def kernel(**inputs):
    import numpy as _np
    import concourse.bacc as _bacc
    from concourse import mybir as _mybir
    from concourse.bass_utils import run_bass_kernel_spmd as _run

    nc = _bacc.Bacc("TRN2", target_bir_lowering=False, num_devices=1)
    arrays = {}

    def given(name):
        a = _np.ascontiguousarray(inputs[name])
        arrays[f"in_{name}_dram"] = a
        return nc.dram_tensor(f"in_{name}_dram", a.shape, _mybir.dt.from_np(a.dtype), kind="ExternalInput").ap()

    x, role_ids, codes = (given(n) for n in _INS)
    l0 = {k: given(f"L0_cond_{v}") for k, v in _L0.items()}
    l1 = {k: given(f"L1_cond_{k}") for k in _ATT}
    l2 = {k: given(f"L2_cond_{k}") for k in _ATT}
    l3 = {k: given(f"L3_cond_{v}") for k, v in _L3.items()}
    out = nc.dram_tensor("out_0_dram", x.shape, _mybir.dt.float32, kind="ExternalOutput").ap()
    build(nc, x, role_ids, codes, l0, l1, l2, l3, out)
    r = _run(nc, [arrays], core_ids=[0])
    return r.results[0]["out_0_dram"]
```
